# Optimizing a Trainium2 kernel written in Bass

```python
import numpy as np
import jax
import jax.numpy as jnp

def _softmax(x, axis=-1):
    return jax.nn.softmax(x, axis=axis)

def _gelu(x):
    return jax.nn.gelu(x, approximate=True)

def _silu(x):
    return jax.nn.silu(x)

def _sigmoid(x):
    return jax.nn.sigmoid(x)

def _layernorm(x, axis=-1, eps=1e-05):
    m = jnp.mean(x, axis=axis, keepdims=True)
    v = jnp.var(x, axis=axis, keepdims=True)
    return (x - m) / jnp.sqrt(v + eps)

def _scatter_add(tgt, idx, src, axis=0):
    return tgt.at[idx].add(src)

def _segment_sum(src, seg, n):
    return jax.ops.segment_sum(src, seg, n)
kernel_name = 'mk_seq_preln_d1_jaxref_r8_e61fa3'

def setup_inputs(seed: int=0):
    np.random.seed(seed)
    _w = jnp.asarray

    def _L0_attn_setup():
        import jax, jax.numpy as jnp
        import numpy as np
        EPS = 1e-06
        CHUNK = 128

        def _feature_map(x):
            return jax.nn.elu(x) + 1.0

        def _linear_attention(q, k, v):
            B, T, D = q.shape
            C = CHUNK
            N = T // C
            qc = q.reshape(B, N, C, D).transpose(1, 0, 2, 3)
            kc = k.reshape(B, N, C, D).transpose(1, 0, 2, 3)
            vc = v.reshape(B, N, C, D).transpose(1, 0, 2, 3)
            mask = jnp.tril(jnp.ones((C, C), bool))

            def step(carry, inp):
                key_sum, kv_sum = carry
                qi, ki, vi = inp
                A = jnp.einsum('bcd,bsd->bcs', qi, ki)
                A = jnp.where(mask, A, 0.0)
                num = jnp.einsum('bcs,bse->bce', A, vi) + jnp.einsum('bcd,bde->bce', qi, kv_sum)
                den = A.sum(-1) + jnp.einsum('bcd,bd->bc', qi, key_sum) + EPS
                out_i = num / den[..., None]
                key_sum = key_sum + ki.sum(1)
                kv_sum = kv_sum + jnp.einsum('bcd,bce->bde', ki, vi)
                return ((key_sum, kv_sum), out_i)
            init = (jnp.zeros((B, D), q.dtype), jnp.zeros((B, D, D), q.dtype))
            (key_sum, kv_sum), out = jax.lax.scan(step, init, (qc, kc, vc))
            out = out.transpose(1, 0, 2, 3).reshape(B, T, D)
            return (out, key_sum, kv_sum)

        def _reference_tuple_inner(chunk, Wq, bq, Wk, bk, Wv, bv, Wo, bo):
            q = _feature_map(chunk @ Wq.T + bq)
            k = _feature_map(chunk @ Wk.T + bk)
            v = chunk @ Wv.T + bv
            attn, key_sum, kv_sum = _linear_attention(q, k, v)
            out = attn @ Wo.T + bo
            return (out, key_sum, kv_sum)
        key = jax.random.key(seed)
        ks = jax.random.split(key, 9)
        B, T, D = (4, 256, 128)
        s = 1.0 / np.sqrt(D)
        f32 = jnp.float32
        return {'chunk': jax.random.normal(ks[0], (B, T, D), f32), 'Wq': jax.random.normal(ks[1], (D, D), f32) * s, 'bq': jnp.zeros((D,), f32), 'Wk': jax.random.normal(ks[2], (D, D), f32) * s, 'bk': jnp.zeros((D,), f32), 'Wv': jax.random.normal(ks[3], (D, D), f32) * s, 'bv': jnp.zeros((D,), f32), 'Wo': jax.random.normal(ks[4], (D, D), f32) * s, 'bo': jnp.zeros((D,), f32)}
    _L0_attn_in = _L0_attn_setup()

    def _L0_ffn_setup():
        import jax, jax.numpy as jnp
        import numpy as np
        E = 8
        TOP_K = 2
        ROUTE_SCALE = 1.0
        ALPHA = 1.702
        LIMIT = 7.0
        D = 128
        F = 128
        B, S = (2, 128)

        def swiglu(h):
            g = jnp.minimum(h[..., ::2], LIMIT)
            l = jnp.clip(h[..., 1::2], -LIMIT, LIMIT)
            return g * jax.nn.sigmoid(ALPHA * g) * (l + 1.0)
        if __name__ == '__main__':
            out = reference(**setup_inputs())
            print(out.shape, out.dtype)
        key = jax.random.key(seed)
        ks = jax.random.split(key, 16)
        sd = 1.0 / np.sqrt(D)
        sf = 1.0 / np.sqrt(F)
        return {'x': jax.random.normal(ks[0], (B, S, D), jnp.float32), 'gate_w': jax.random.normal(ks[1], (E, D), jnp.float32) * sd, 'gate_b': jax.random.normal(ks[2], (E,), jnp.float32) * 0.01, 'w1': jax.random.normal(ks[3], (E, 2 * F, D), jnp.float32) * sd, 'b1': jax.random.normal(ks[4], (E, 2 * F), jnp.float32) * 0.01, 'w3': jax.random.normal(ks[5], (E, 2 * F, D), jnp.float32) * sd, 'b3': jax.random.normal(ks[6], (E, 2 * F), jnp.float32) * 0.01, 'w2': jax.random.normal(ks[7], (E, D, F), jnp.float32) * sf, 'b2': jax.random.normal(ks[8], (E, D), jnp.float32) * 0.01, 'sw1': jax.random.normal(ks[9], (2 * F, D), jnp.float32) * sd, 'sb1': jax.random.normal(ks[10], (2 * F,), jnp.float32) * 0.01, 'sw3': jax.random.normal(ks[11], (2 * F, D), jnp.float32) * sd, 'sb3': jax.random.normal(ks[12], (2 * F,), jnp.float32) * 0.01, 'sw2': jax.random.normal(ks[13], (D, F), jnp.float32) * sf, 'sb2': jax.random.normal(ks[14], (D,), jnp.float32) * 0.01}
    _L0_ffn_in = _L0_ffn_setup()
    _d = {'L0_attn_chunk': _L0_attn_in['chunk'], 'L0_attn_Wq': _L0_attn_in['Wq'], 'L0_attn_bq': _L0_attn_in['bq'], 'L0_attn_Wk': _L0_attn_in['Wk'], 'L0_attn_bk': _L0_attn_in['bk'], 'L0_attn_Wv': _L0_attn_in['Wv'], 'L0_attn_bv': _L0_attn_in['bv'], 'L0_attn_Wo': _L0_attn_in['Wo'], 'L0_attn_bo': _L0_attn_in['bo'], 'L0_ffn_gate_w': _L0_ffn_in['gate_w'], 'L0_ffn_gate_b': _L0_ffn_in['gate_b'], 'L0_ffn_w1': _L0_ffn_in['w1'], 'L0_ffn_b1': _L0_ffn_in['b1'], 'L0_ffn_w3': _L0_ffn_in['w3'], 'L0_ffn_b3': _L0_ffn_in['b3'], 'L0_ffn_w2': _L0_ffn_in['w2'], 'L0_ffn_b2': _L0_ffn_in['b2'], 'L0_ffn_sw1': _L0_ffn_in['sw1'], 'L0_ffn_sb1': _L0_ffn_in['sb1'], 'L0_ffn_sw3': _L0_ffn_in['sw3'], 'L0_ffn_sb3': _L0_ffn_in['sb3'], 'L0_ffn_sw2': _L0_ffn_in['sw2'], 'L0_ffn_sb2': _L0_ffn_in['sb2']}
    _x0 = _d['L0_attn_chunk']
    _d['L0_attn_chunk'] = jax.random.normal(jax.random.fold_in(jax.random.key(seed), 1), (16, 512, 128), dtype=_x0.dtype)
    del _x0
    return _d

def reference(L0_attn_chunk, L0_attn_Wq, L0_attn_bq, L0_attn_Wk, L0_attn_bk, L0_attn_Wv, L0_attn_bv, L0_attn_Wo, L0_attn_bo, L0_ffn_gate_w, L0_ffn_gate_b, L0_ffn_w1, L0_ffn_b1, L0_ffn_w3, L0_ffn_b3, L0_ffn_w2, L0_ffn_b2, L0_ffn_sw1, L0_ffn_sb1, L0_ffn_sw3, L0_ffn_sb3, L0_ffn_sw2, L0_ffn_sb2):

    def _L0_attn_ref(chunk, Wq, bq, Wk, bk, Wv, bv, Wo, bo):
        import jax, jax.numpy as jnp
        import numpy as np
        EPS = 1e-06
        CHUNK = 128

        def _feature_map(x):
            return jax.nn.elu(x) + 1.0

        def _linear_attention(q, k, v):
            B, T, D = q.shape
            C = CHUNK
            N = T // C
            qc = q.reshape(B, N, C, D).transpose(1, 0, 2, 3)
            kc = k.reshape(B, N, C, D).transpose(1, 0, 2, 3)
            vc = v.reshape(B, N, C, D).transpose(1, 0, 2, 3)
            mask = jnp.tril(jnp.ones((C, C), bool))

            def step(carry, inp):
                key_sum, kv_sum = carry
                qi, ki, vi = inp
                A = jnp.einsum('bcd,bsd->bcs', qi, ki)
                A = jnp.where(mask, A, 0.0)
                num = jnp.einsum('bcs,bse->bce', A, vi) + jnp.einsum('bcd,bde->bce', qi, kv_sum)
                den = A.sum(-1) + jnp.einsum('bcd,bd->bc', qi, key_sum) + EPS
                out_i = num / den[..., None]
                key_sum = key_sum + ki.sum(1)
                kv_sum = kv_sum + jnp.einsum('bcd,bce->bde', ki, vi)
                return ((key_sum, kv_sum), out_i)
            init = (jnp.zeros((B, D), q.dtype), jnp.zeros((B, D, D), q.dtype))
            (key_sum, kv_sum), out = jax.lax.scan(step, init, (qc, kc, vc))
            out = out.transpose(1, 0, 2, 3).reshape(B, T, D)
            return (out, key_sum, kv_sum)

        def _reference_tuple_inner(chunk, Wq, bq, Wk, bk, Wv, bv, Wo, bo):
            q = _feature_map(chunk @ Wq.T + bq)
            k = _feature_map(chunk @ Wk.T + bk)
            v = chunk @ Wv.T + bv
            attn, key_sum, kv_sum = _linear_attention(q, k, v)
            out = attn @ Wo.T + bo
            return (out, key_sum, kv_sum)
        return _reference_tuple_inner(chunk, Wq, bq, Wk, bk, Wv, bv, Wo, bo)[0]

    def _L0_ffn_ref(x, gate_w, gate_b, w1, b1, w3, b3, w2, b2, sw1, sb1, sw3, sb3, sw2, sb2):
        import jax, jax.numpy as jnp
        import numpy as np
        E = 8
        TOP_K = 2
        ROUTE_SCALE = 1.0
        ALPHA = 1.702
        LIMIT = 7.0
        D = 128
        F = 128
        B, S = (2, 128)

        def swiglu(h):
            g = jnp.minimum(h[..., ::2], LIMIT)
            l = jnp.clip(h[..., 1::2], -LIMIT, LIMIT)
            return g * jax.nn.sigmoid(ALPHA * g) * (l + 1.0)
        if __name__ == '__main__':
            out = reference(**setup_inputs())
            print(out.shape, out.dtype)
        inp_shape = x.shape
        xt = x.reshape(-1, D)
        logits = xt @ gate_w.T
        scores = jax.nn.softmax(logits.astype(jnp.float32), axis=-1)
        biased = scores + gate_b.astype(jnp.float32)
        idx = jax.lax.top_k(biased, TOP_K)[1]
        weights = (jnp.take_along_axis(scores, idx, axis=-1) * ROUTE_SCALE).astype(x.dtype)
        cw = jnp.sum(jax.nn.one_hot(idx, E, dtype=x.dtype) * weights[..., None], axis=1)
        h1 = jnp.einsum('td,efd->etf', xt, w1) + b1[:, None, :]
        h3 = jnp.einsum('td,efd->etf', xt, w3) + b3[:, None, :]
        a = swiglu(h1 * h3)
        y = jnp.einsum('etf,edf->etd', a, w2) + b2[:, None, :]
        routed = jnp.einsum('te,etd->td', cw, y)
        sh = swiglu((xt @ sw1.T + sb1) * (xt @ sw3.T + sb3))
        shared = sh @ sw2.T + sb2
        return (routed + shared).reshape(inp_shape)
    x = L0_attn_chunk
    x = x + _L0_attn_ref(_layernorm(x, axis=-1), L0_attn_Wq, L0_attn_bq, L0_attn_Wk, L0_attn_bk, L0_attn_Wv, L0_attn_bv, L0_attn_Wo, L0_attn_bo)
    x = x + _L0_ffn_ref(_layernorm(x, axis=-1), L0_ffn_gate_w, L0_ffn_gate_b, L0_ffn_w1, L0_ffn_b1, L0_ffn_w3, L0_ffn_b3, L0_ffn_w2, L0_ffn_b2, L0_ffn_sw1, L0_ffn_sb1, L0_ffn_sw3, L0_ffn_sb3, L0_ffn_sw2, L0_ffn_sb2)
    return x

_drawn_inputs = setup_inputs


def setup_inputs(seed=0):
    import zlib

    import numpy as np

    out = dict(_drawn_inputs(seed))
    spreads = {'L0_attn_bq': (0.0, 0.8),
     'L0_attn_bk': (0.0, 0.8),
     'L0_attn_bv': (0.0, 0.1),
     'L0_attn_bo': (0.0, 0.1)}
    factors = {'L0_attn_Wq': 4.611,
     'L0_attn_Wk': 3.299,
     'L0_ffn_b1': 8.0,
     'L0_ffn_b3': 8.0,
     'L0_ffn_b2': 8.0,
     'L0_ffn_sb1': 6.854,
     'L0_ffn_sb3': 7.427,
     'L0_ffn_sb2': 8.0}
    for name, (base, spread) in spreads.items():
        noise = np.random.default_rng([zlib.crc32(name.encode()), seed]).standard_normal(out[name].shape)
        drawn = base * np.exp(spread * noise) if base else spread * noise
        out[name] = jnp.asarray(drawn.astype(out[name].dtype))
    for name, factor in factors.items():
        out[name] = (out[name] * factor).astype(out[name].dtype)
    return out
```

```python
from contextlib import ExitStack

import concourse.bass as bass
from concourse import mybir

F32 = mybir.dt.float32
F32R = mybir.dt.float32r
ACT = mybir.ActivationFunctionType
ALU = mybir.AluOpType
AX_X = mybir.AxisListType.X

P = 128
D = 128
TOK = 512
CH = TOK // P
NR = 8
NE = NR + 1
LIMIT = 7.0
LN_EPS = 1e-5
DEN_EPS = 1e-6
LN_STEPS = 5
BIG = 1e30

C_BUP, C_BQ, C_BK, C_BV, C_SB2, N_COL = 0, 4 * NE, 4 * NE + 1, 4 * NE + 2, 4 * NE + 3, 4 * NE + 4


def block_kernel(nc, x_in, w_up, w_down, attn_w, cols, rows, gate_w, b2rows, out):
    NB = x_in.shape[0] // TOK
    x_b = x_in.rearrange("(b c p) d -> b p c d", c=CH, p=P)
    out_b = out.rearrange("(b c p) d -> b p c d", c=CH, p=P)

    with ExitStack() as ctx:
        def sb(name, shape, dt=F32):
            return ctx.enter_context(nc.sbuf_tensor(name, shape, dt))

        def bank(name):
            return ctx.enter_context(nc.psum_tensor(name, [P, TOK], F32))

        def sem(name):
            return ctx.enter_context(nc.semaphore(name))

        up_f32 = sb("up_f32", [P, NE, 4, P])
        down_f32 = sb("down_f32", [P, NE, D])
        up_hi, up_lo = sb("up_hi", [P, NE, 4, P], F32R), sb("up_lo", [P, NE, 4, P], F32R)
        down_hi, down_lo = sb("down_hi", [P, NE, D], F32R), sb("down_lo", [P, NE, D], F32R)
        attn_sb = sb("attn_sb", [P, 4, P])
        wov = sb("wov", [P, D])
        bvo = sb("bvo", [P, D])
        bv_wide = sb("bv_wide", [P, P])
        col = sb("col", [P, N_COL])
        row = sb("row", [P, D + NR])
        gate_f32 = sb("gate_f32", [P, NR])
        gate_hi, gate_lo = sb("gate_hi", [P, NR], F32R), sb("gate_lo", [P, NR], F32R)
        b2_f32 = sb("b2_f32", [2 * NR, D])
        b2_hi, b2_lo = sb("b2_hi", [2 * NR, D], F32R), sb("b2_lo", [2 * NR, D], F32R)
        ident = sb("ident", [P, P])
        causal = sb("causal", [P, P])
        pick_f32 = sb("pick_f32", [2 * NR, NR, P])
        pick = sb("pick", [2 * NR, NR, P], F32R)
        rank = sb("rank", [P, NR])
        minus_half = sb("minus_half", [P, CH])

        x_sb = [sb(f"x_sb{i}", [P, CH, D]) for i in range(2)]
        stats1, mv1 = sb("stats1", [P, CH, 6]), sb("mv1", [P, 6, CH])
        stats2, mv2 = sb("stats2", [P, CH, 6]), sb("mv2", [P, 6, CH])
        var1, rstd1 = sb("var1", [P, CH]), sb("rstd1", [P, CH])
        var2, rstd2 = sb("var2", [P, CH]), sb("rstd2", [P, CH])
        xn = sb("xn", [P, CH, D])
        xnT = sb("xnT", [P, TOK])
        q_exp, q_relu, qf = sb("q_exp", [P, TOK]), sb("q_relu", [P, TOK]), sb("qf", [P, TOK])
        k_exp, k_relu, kf = sb("k_exp", [P, TOK]), sb("k_relu", [P, TOK]), sb("kf", [P, TOK])
        v1 = sb("v1", [P, CH, D + 1])
        a_diag = sb("a_diag", [P, CH, P])
        a_off = sb("a_off", [P, 6, P])
        x_bo = sb("x_bo", [P, CH, D])
        den, rden = sb("den", [P, CH]), sb("rden", [P, CH])
        y_sb = [sb(f"y_sb{i}", [P, CH, D]) for i in range(2)]
        yn = sb("yn", [P, CH, D])
        ynT_hi = [sb(f"ynT_hi{i}", [P, TOK], F32R) for i in range(2)]
        ynT_lo = [sb(f"ynT_lo{i}", [P, TOK], F32R) for i in range(2)]

        r_max, r_lg, r_ex = sb("r_max", [P, CH]), sb("r_lg", [P, CH, NR]), sb("r_ex", [P, CH, NR])
        r_sum, r_inv, r_sc = sb("r_sum", [P, CH]), sb("r_inv", [P, CH]), sb("r_sc", [P, CH, NR])
        r_b, r_m = sb("r_b", [P, CH, NR]), sb("r_m", [P, 2, CH])
        r_eq, r_w = sb("r_eq", [P, 2, CH, NR]), sb("r_w", [P, 2, CH, NR])
        r_f, r_oh = sb("r_f", [P, 2, CH]), sb("r_oh", [P, 2, CH, NR])
        r_b2, r_sel, r_cw = sb("r_b2", [P, CH, NR]), sb("r_sel", [P, CH, NR]), sb("r_cw", [P, CH, NR])
        cw_parts = sb("cw_parts", [P, CH, 2 * NR], F32R)
        cwT = [sb(f"cwT{i}", [2 * NR, TOK], F32R) for i in range(2)]

        h3_sb = [[sb(f"h3_sb{i}{h}", [P, TOK]) for h in "gl"] for i in range(2)]
        gate_act = [sb(f"gate_act{i}", [P, TOK]) for i in range(2)]
        lin = [sb(f"lin{i}", [P, TOK]) for i in range(2)]
        glu = [sb(f"glu{i}", [P, TOK]) for i in range(2)]
        cw_wide = [sb(f"cw_wide{i}", [P, TOK]) for i in range(2)]
        glu_w = [sb(f"glu_w{i}", [P, TOK]) for i in range(2)]
        act = [sb(f"act{i}", [P, TOK]) for i in range(2)]
        act_hi = [sb(f"act_hi{i}", [P, TOK], F32R) for i in range(2)]
        act_lo = [sb(f"act_lo{i}", [P, TOK], F32R) for i in range(2)]
        ffT = sb("ffT", [P, TOK])
        o_sb = [sb(f"o_sb{i}", [P, CH, D]) for i in range(2)]

        h_bank = [bank(f"h_bank{k}") for k in range(4)]
        ff_bank = bank("ff_bank")
        cw_bank = bank("cw_bank")
        at_bank = [bank(f"at_bank{k}") for k in range(2)]

        w_loaded = [sem(f"w_loaded{e}") for e in range(NE)]
        c_loaded, aw_loaded = sem("c_loaded"), sem("aw_loaded")
        x_loaded = [sem("x_loaded0"), sem("x_loaded1")]
        o_stored = [sem("o_stored0"), sem("o_stored1")]
        pool_const, dve_const = sem("pool_const"), sem("dve_const")
        w_hi_done, w_lo_done = sem("w_hi_done"), sem("w_lo_done")
        wov_mm, wov_ready = sem("wov_mm"), sem("wov_ready")
        ln1_step, ln2_step, route_step, den_step = (sem("ln1_step"), sem("ln2_step"),
                                                    sem("route_step"), sem("den_step"))
        rstd1_done, rstd2_done = sem("rstd1_done"), sem("rstd2_done")
        xn_ready, t1_done, xnT_ready = sem("xn_ready"), sem("t1_done"), sem("xnT_ready")
        q_mm, k_mm, v_mm = sem("q_mm"), sem("k_mm"), sem("v_mm")
        q_read, k_read = sem("q_read"), sem("k_read")
        qk_ready, v_ready = sem("qk_ready"), sem("v_ready")
        diag_mm, off_mm, off2_mm = sem("diag_mm"), sem("off_mm"), sem("off2_mm")
        diag_ready, off_ready, off2_ready = sem("diag_ready"), sem("off_ready"), sem("off2_ready")
        xbo_ready, num_mm, y_ready = sem("xbo_ready"), sem("num_mm"), sem("y_ready")
        yn_ready, t2_done = sem("yn_ready"), sem("t2_done")
        ynT_hi_ready, ynT_lo_ready = sem("ynT_hi_ready"), sem("ynT_lo_ready")
        gate_mm, lg_ready, ex_ready = sem("gate_mm"), sem("lg_ready"), sem("ex_ready")
        cw_ready, cwT_mm, cwT_ready = sem("cw_ready"), sem("cwT_mm"), sem("cwT_ready")
        h_ready, h3_copied, h_used = sem("h_ready"), sem("h3_copied"), sem("h_used")
        ga_ready, lin_ready, glu_ready = sem("ga_ready"), sem("lin_ready"), sem("glu_ready")
        cw_mm, cw_copied, gluw_ready = sem("cw_mm"), sem("cw_copied"), sem("gluw_ready")
        act_ready, act_hi_ready, act_lo_ready = sem("act_ready"), sem("act_hi_ready"), sem("act_lo_ready")
        down_done, ff_copied = sem("down_done"), sem("ff_copied")
        ffo_mm, o_ready = sem("ffo_mm"), sem("o_ready")

        OFF = [(0, 1), (0, 2), (0, 3), (2, 3), (1, 2), (1, 3)]

        def walk(eng, body):
            body(-1, -1, 1, False, False, True, True)
            body(0, 0, 0, True, False, True, True)
            with eng.Fori(0, (NB - 4) // 2) as i:
                body(2 * i + 1, i, 1, True, True, True, True)
                body(2 * i + 2, i + 1, 0, True, True, True, True)
            body(NB - 3, (NB - 3) // 2, 1, True, True, True, True)
            body(NB - 2, (NB - 2) // 2, 0, True, True, True, False)
            body(NB - 1, (NB - 1) // 2, 1, True, True, False, False)
            body(NB, NB // 2, 0, False, True, False, False)

        block = ctx.enter_context(nc.Block())

        @block.sync
        def _(sp):
            sp.dma_start(x_sb[0][:], x_b[0]).then_inc(x_loaded[0], 16)
            sp.dma_start(col[:], cols).then_inc(c_loaded, 16)
            sp.dma_start(attn_sb[:], attn_w).then_inc(aw_loaded, 16)
            sp.dma_start(row[:], rows).then_inc(c_loaded, 16)
            sp.dma_start(gate_f32[:], gate_w).then_inc(c_loaded, 16)
            sp.dma_start(b2_f32[:], b2rows).then_inc(c_loaded, 16)
            sp.dma_start(x_sb[1][:], x_b[1]).then_inc(x_loaded[1], 16)
            for e in range(NE):
                sp.dma_start(up_f32[:, e], w_up[:, e]).then_inc(w_loaded[e], 16)
                sp.dma_start(down_f32[:, e], w_down[:, e]).then_inc(w_loaded[e], 16)

            def body(n, h, par, ff, old, att, nxt):
                if nxt and not (isinstance(n, int) and n + 3 >= NB):
                    sp.wait_ge(xbo_ready, n + 2)
                    sp.dma_start(x_sb[1 - par][:], x_b[n + 3]).then_inc(x_loaded[1 - par], 16)
                if old:
                    sp.wait_ge(o_ready, n)
                    sp.dma_start(out_b[n - 1], o_sb[1 - par][:]).then_inc(o_stored[1 - par], 16)

            walk(sp, body)
            for i in range(2):
                sp.wait_ge(o_stored[i], 16 * (NB // 2))

        @block.scalar
        def _(act_e):
            def split_hi(e):
                act_e.wait_ge(w_loaded[e], 32)
                act_e.activation(up_hi[:, e], up_f32[:, e], ACT.Copy).then_inc(w_hi_done, 1)
                act_e.activation(down_hi[:, e], down_f32[:, e], ACT.Copy).then_inc(w_hi_done, 1)

            act_e.wait_ge(wov_mm, 1)
            act_e.activation(wov[:], at_bank[1][:, 0:D], ACT.Copy).then_inc(wov_ready, 1)
            act_e.activation(bvo[:], at_bank[1][:, D:2 * D], ACT.Copy).then_inc(wov_ready, 1)

            def body(n, h, par, ff, old, att, nxt):
                m = n + 1
                for e in range(NE):
                    u, r = 9 * n + e, (par + e) % 2
                    if ff and e > 0 or old and e == 0:
                        act_e.wait_ge(act_ready, u)
                        if not (isinstance(u, int) and u < 3):
                            act_e.wait_ge(down_done, u - 2)
                        act_e.activation(act_hi[1 - r][:], act[1 - r][:], ACT.Copy).then_inc(act_hi_ready, 1)
                    if ff:
                        act_e.wait_ge(h_ready, 4 * u + 1)
                        act_e.activation(h3_sb[r][0][:], h_bank[0][:], ACT.Identity,
                                         bias=col[:, 4 * e:4 * e + 1]).then_inc(h3_copied, 1)
                    if att and e == 0:
                        act_e.wait_ge(t1_done, m + 1)
                        act_e.activation(xnT[:], at_bank[0][:], ACT.Copy).then_inc(xnT_ready, 1)
                    if att and e == 7:
                        act_e.wait_ge(t2_done, m + 1)
                        act_e.activation(ynT_hi[1 - par][:], at_bank[1][:], ACT.Copy).then_inc(ynT_hi_ready, 1)
                    if ff and e == 1:
                        act_e.wait_ge(cwT_mm, n + 1)
                        act_e.activation(cwT[par][:], cw_bank[0:2 * NR, :], ACT.Copy).then_inc(cwT_ready, 1)
                    if ff and e >= 1:
                        act_e.wait_ge(cw_mm, NR * n + e)
                        act_e.activation(cw_wide[r][:], cw_bank[:], ACT.Copy).then_inc(cw_copied, 1)
                    if ff:
                        act_e.wait_ge(h_ready, 4 * u + 3)
                        act_e.activation(h3_sb[r][1][:], h_bank[2][:], ACT.Identity,
                                         bias=col[:, 4 * e + 2:4 * e + 3]).then_inc(h3_copied, 1)
                        act_e.wait_ge(ga_ready, u + 1)
                        act_e.activation(glu[r][:], gate_act[r][:],
                                         ACT.Gelu_apprx_sigmoid).then_inc(glu_ready, 1)
                    if old and e == 2:
                        act_e.wait_ge(down_done, NE * n)
                        act_e.activation(ffT[:], ff_bank[:], ACT.Identity,
                                         bias=col[:, C_SB2:C_SB2 + 1]).then_inc(ff_copied, 1)
                    if att and e == 1:
                        act_e.wait_ge(q_mm, m + 1)
                        act_e.activation(q_exp[:], at_bank[1][:], ACT.Exp,
                                         bias=col[:, C_BQ:C_BQ + 1]).then_inc(q_read, 1)
                        act_e.activation(q_relu[:], at_bank[1][:], ACT.Relu,
                                         bias=col[:, C_BQ:C_BQ + 1]).then_inc(q_read, 1)
                        act_e.wait_ge(k_mm, m + 1)
                        act_e.activation(k_exp[:], at_bank[0][:], ACT.Exp,
                                         bias=col[:, C_BK:C_BK + 1]).then_inc(k_read, 1)
                        act_e.activation(k_relu[:], at_bank[0][:], ACT.Relu,
                                         bias=col[:, C_BK:C_BK + 1]).then_inc(k_read, 1)
                    if att and e == 3:
                        act_e.wait_ge(off_mm, m + 1)
                        act_e.activation(a_off[:, 0:4], at_bank[1][:].rearrange("p (k t) -> p k t", t=P),
                                         ACT.Copy).then_inc(off_ready, 1)
                    if att and e == 4:
                        act_e.wait_ge(off2_mm, m + 1)
                        act_e.activation(a_off[:, 4:6], at_bank[0][:, 0:2 * P].rearrange("p (k t) -> p k t", t=P),
                                         ACT.Copy).then_inc(off2_ready, 1)
                    if att and e == 8:
                        act_e.wait_ge(lg_ready, m + 1)
                        act_e.activation(r_ex[:], r_lg[:], ACT.Exp).then_inc(ex_ready, 1)
                    if isinstance(n, int) and n == -1:
                        split_hi(e)

            walk(act_e, body)

        @block.vector
        def _(dve):
            def chunk_bc(small):
                return small.unsqueeze(2).to_broadcast([P, CH, NR])

            def norm_stats(src, stats, mv, var, step, m, x_wait=None):
                if x_wait is not None:
                    dve.wait_ge(*x_wait)
                for c in range(CH):
                    i = dve.bn_stats(stats[:, c], src[:, c])
                i.then_inc(step, 1)
                dve.wait_ge(step, LN_STEPS * m + 1)
                dve.tensor_tensor(mv[:, 0], stats[:, :, 1], stats[:, :, 4], ALU.add)
                dve.tensor_tensor(mv[:, 1], stats[:, :, 1], stats[:, :, 4], ALU.subtract)
                dve.tensor_tensor(mv[:, 2], stats[:, :, 2], stats[:, :, 5], ALU.add).then_inc(step, 1)
                dve.wait_ge(step, LN_STEPS * m + 2)
                dve.tensor_scalar(mv[:, 3], mv[:, 0], 0.5, None, ALU.mult)
                dve.scalar_tensor_tensor(mv[:, 4], mv[:, 1], 0.25, mv[:, 1], ALU.mult, ALU.mult).then_inc(step, 1)
                dve.wait_ge(step, LN_STEPS * m + 3)
                dve.tensor_scalar(mv[:, 5], mv[:, 4], LN_EPS, None, ALU.add).then_inc(step, 1)
                dve.wait_ge(step, LN_STEPS * m + 4)
                dve.scalar_tensor_tensor(var[:], mv[:, 2], 1.0 / D, mv[:, 5], ALU.mult, ALU.add).then_inc(step, 1)

            def normalize(dst, src, mv, rstd, ready):
                for c in range(CH):
                    i = dve.tensor_scalar(dst[:, c], src[:, c], mv[:, 3, c:c + 1], rstd[:, c:c + 1],
                                          ALU.subtract, ALU.mult)
                i.then_inc(ready, 1)

            dve.wait_ge(c_loaded, 64)
            dve.tensor_copy(bv_wide[:], col[:, C_BV:C_BV + 1].to_broadcast([P, P])).then_inc(dve_const, 1)
            dve.tensor_copy(gate_hi[:], gate_f32[:]).then_inc(dve_const, 1)
            dve.tensor_copy(b2_hi[:], b2_f32[:]).then_inc(dve_const, 1)
            norm_stats(x_sb[0], stats1, mv1, var1, ln1_step, 0, (x_loaded[0], 16))
            dve.wait_ge(dve_const, 3)
            dve.tensor_tensor(gate_lo[:], gate_f32[:], gate_hi[:].bitcast(F32), ALU.subtract).then_inc(dve_const, 1)
            dve.tensor_tensor(b2_lo[:], b2_f32[:], b2_hi[:].bitcast(F32), ALU.subtract).then_inc(dve_const, 1)
            dve.wait_ge(pool_const, 9)
            dve.tensor_copy(pick[:], pick_f32[:]).then_inc(dve_const, 1)
            dve.wait_ge(rstd1_done, 1)
            normalize(xn, x_sb[0], mv1, rstd1, xn_ready)

            def routing_scores(m):
                dve.wait_ge(gate_mm, m + 1)
                lg = at_bank[0][:, 0:CH * NR].rearrange("p (c r) -> p c r", r=NR)
                dve.reduce_max(r_max[:], lg, AX_X).then_inc(route_step, 1)
                dve.wait_ge(route_step, 19 * m + 1)
                dve.tensor_tensor(r_lg[:], lg, chunk_bc(r_max[:]), ALU.subtract).then_inc(lg_ready, 1)

            def routing_choice(m):
                step = [1]

                def link(ins):
                    step[0] += 1
                    ins.then_inc(route_step, 1)
                    dve.wait_ge(route_step, 19 * m + step[0])

                dve.wait_ge(ex_ready, m + 1)
                link(dve.reduce_sum(r_sum[:], r_ex[:], AX_X))
                link(dve.reciprocal(r_inv[:], r_sum[:]))
                link(dve.tensor_tensor(r_sc[:], r_ex[:], chunk_bc(r_inv[:]), ALU.mult))
                link(dve.tensor_tensor(r_b[:], r_sc[:], row[:, D:D + NR].unsqueeze(1).to_broadcast([P, CH, NR]), ALU.add))
                for k, src in enumerate((r_b, r_b2)):
                    link(dve.reduce_max(r_m[:, k], src[:], AX_X))
                    link(dve.tensor_tensor(r_eq[:, k], src[:], chunk_bc(r_m[:, k]), ALU.is_equal))
                    link(dve.tensor_tensor(r_w[:, k], r_eq[:, k], rank[:].unsqueeze(1).to_broadcast([P, CH, NR]), ALU.mult))
                    link(dve.reduce_max(r_f[:, k], r_w[:, k], AX_X))
                    link(dve.tensor_tensor(r_oh[:, k], r_w[:, k], chunk_bc(r_f[:, k]), ALU.is_equal))
                    if k == 0:
                        link(dve.scalar_tensor_tensor(r_b2[:], r_oh[:, 0], -BIG, r_b[:], ALU.mult, ALU.add))
                link(dve.tensor_tensor(r_sel[:], r_oh[:, 0], r_oh[:, 1], ALU.add))
                link(dve.tensor_tensor(r_cw[:], r_sel[:], r_sc[:], ALU.mult))
                link(dve.tensor_copy(cw_parts[:, :, 0:NR], r_cw[:]))
                assert step[0] == 19
                dve.tensor_tensor(cw_parts[:, :, NR:2 * NR], r_cw[:], cw_parts[:, :, 0:NR].bitcast(F32),
                                  ALU.subtract).then_inc(cw_ready, 1)

            def body(n, h, par, ff, old, att, nxt):
                m = n + 1
                for e in range(NE):
                    u, r = 9 * n + e, (par + e) % 2
                    if ff and e > 0 or old and e == 0:
                        dve.wait_ge(lin_ready, u)
                        if e == 1:
                            dve.wait_ge(glu_ready, u)
                            if not (isinstance(u, int) and u < 3):
                                dve.wait_ge(act_lo_ready, u - 2)
                            src = glu
                        else:
                            dve.wait_ge(gluw_ready, NR * n + (e - 1 if e else 0))
                            src = glu_w
                        dve.scalar_tensor_tensor(act[1 - r][:], lin[1 - r][:], 1.0, src[1 - r][:],
                                                 ALU.add, ALU.mult).then_inc(act_ready, 1)
                    if ff:
                        dve.wait_ge(h3_copied, 2 * u + 1)
                        dve.wait_ge(h_ready, 4 * u + 2)
                        dve.scalar_tensor_tensor(gate_act[r][:], h_bank[1][:], col[:, 4 * e + 1:4 * e + 2],
                                                 h3_sb[r][0][:], ALU.add, ALU.mult).then_inc(h_used, 1)
                    if ff and e == 0:
                        routing_choice(n)
                    if att and e == 2:
                        dve.wait_ge(q_read, 2 * m + 2)
                        dve.scalar_tensor_tensor(qf[:], q_exp[:], 1.0, q_relu[:], ALU.min, ALU.add).then_inc(qk_ready, 1)
                        dve.wait_ge(k_read, 2 * m + 2)
                        dve.scalar_tensor_tensor(kf[:], k_exp[:], 1.0, k_relu[:], ALU.min, ALU.add).then_inc(qk_ready, 1)
                    if att and e == 2:
                        dve.wait_ge(v_mm, m + 1)
                        if isinstance(n, int) and n == -1:
                            dve.wait_ge(wov_ready, 2)
                        dve.tensor_tensor(v1[:, :, 0:D], at_bank[1][:].rearrange("p (c d) -> p c d", d=D),
                                          bvo[:].unsqueeze(1).to_broadcast([P, CH, D]), ALU.add).then_inc(v_ready, 1)
                    if att and e == 3:
                        dve.wait_ge(diag_mm, m + 1)
                        dve.tensor_tensor(a_diag[:], at_bank[0][:].rearrange("p (c t) -> p c t", t=P),
                                          causal[:].unsqueeze(1).to_broadcast([P, CH, P]), ALU.mult).then_inc(diag_ready, 1)
                    if old and e == 3:
                        dve.wait_ge(ffo_mm, n)
                        if not (isinstance(n, int) and n < 3):
                            dve.wait_ge(o_stored[1 - par], 16 * (h - (1 if par == 0 else 0)))
                        dve.tensor_tensor(o_sb[1 - par][:], cw_bank[:].rearrange("p (c d) -> p c d", d=D),
                                          y_sb[1 - par][:], ALU.add).then_inc(o_ready, 1)
                    if att and e == 5:
                        dve.wait_ge(xbo_ready, m + 1)
                        for g in range(2):
                            o = at_bank[1 - g][:, 0:2 * (D + 1)].rearrange("p (c d) -> p c d", d=D + 1)
                            dve.wait_ge(num_mm, 2 * m + g + 1)
                            dve.tensor_scalar(den[:, 2 * g:2 * g + 2], o[:, :, D], DEN_EPS, None, ALU.add).then_inc(den_step, 1)
                            dve.wait_ge(den_step, 4 * m + 2 * g + 1)
                            dve.reciprocal(rden[:, 2 * g:2 * g + 2], den[:, 2 * g:2 * g + 2]).then_inc(den_step, 1)
                            dve.wait_ge(den_step, 4 * m + 2 * g + 2)
                            for c in range(2):
                                dve.scalar_tensor_tensor(y_sb[1 - par][:, 2 * g + c], o[:, c, 0:D],
                                                         rden[:, 2 * g + c:2 * g + c + 1], x_bo[:, 2 * g + c],
                                                         ALU.mult, ALU.add).then_inc(y_ready, 1)
                        norm_stats(y_sb[1 - par], stats2, mv2, var2, ln2_step, m, (y_ready, 4 * m + 4))
                    if att and e == 6:
                        dve.wait_ge(rstd2_done, m + 1)
                        normalize(yn, y_sb[1 - par], mv2, rstd2, yn_ready)
                    if att and e == 7:
                        dve.wait_ge(t2_done, m + 1)
                        dve.wait_ge(ynT_hi_ready, m + 1)
                        dve.tensor_tensor(ynT_lo[1 - par][:], at_bank[1][:], ynT_hi[1 - par][:].bitcast(F32),
                                          ALU.subtract).then_inc(ynT_lo_ready, 1)
                    if ff:
                        dve.wait_ge(h_used, 2 * u + 1)
                        dve.tensor_scalar(gate_act[r][:], gate_act[r][:], LIMIT, None, ALU.min).then_inc(ga_ready, 1)
                        dve.wait_ge(h3_copied, 2 * u + 2)
                        dve.wait_ge(h_ready, 4 * u + 4)
                        dve.scalar_tensor_tensor(lin[r][:], h_bank[3][:], col[:, 4 * e + 3:4 * e + 4],
                                                 h3_sb[r][1][:], ALU.add, ALU.mult).then_inc(h_used, 1)
                    if nxt and e == 7:
                        norm_stats(x_sb[par], stats1, mv1, var1, ln1_step, m + 1, (x_loaded[par], 16 * (h + 2)))
                    if att and e == 8:
                        routing_scores(m)
                    if nxt and e == 8:
                        dve.wait_ge(rstd1_done, m + 2)
                        normalize(xn, x_sb[par], mv1, rstd1, xn_ready)
                    if ff:
                        dve.wait_ge(h_used, 2 * u + 2)
                        dve.tensor_scalar(lin[r][:], lin[r][:], LIMIT, -LIMIT, ALU.min, ALU.max).then_inc(lin_ready, 1)

            walk(dve, body)

        @block.gpsimd
        def _(pool):
            def ones_where_zero(t, base, pattern, chan, count):
                pool.wait_ge(pool_const, count)
                pool.affine_select(out=t, in_=t, compare_op=ALU.not_equal, fill=1.0, base=base,
                                   pattern=pattern, channel_multiplier=chan).then_inc(pool_const, 1)

            pool.memset(minus_half[:], -0.5).then_inc(pool_const, 1)
            pool.memset(ident[:], 0.0).then_inc(pool_const, 1)
            pool.memset(causal[:], 1.0).then_inc(pool_const, 1)
            pool.memset(pick_f32[:], 0.0).then_inc(pool_const, 1)
            pool.memset(v1[:], 1.0).then_inc(pool_const, 1)
            ones_where_zero(ident[:], 0, [[-1, P]], 1, 2)
            ones_where_zero(pick_f32[:], 0, [[-1, NR], [0, P]], 1, 4)
            ones_where_zero(pick_f32[:], -NR, [[-1, NR], [0, P]], 1, 7)
            pool.iota(rank[:], pattern=[[-1, NR]], base=NR, channel_multiplier=0,
                      allow_small_or_imprecise_dtypes=True).then_inc(pool_const, 1)
            pool.affine_select(out=causal[:], in_=causal[:], compare_op=ALU.is_ge, fill=0.0, base=0,
                               pattern=[[1, P]], channel_multiplier=-1).then_inc(pool_const, 1)

            def rsqrt(var, rstd, step, count, done):
                pool.wait_ge(step, count)
                pool.tensor_tensor(rstd[:], var[:], minus_half[:], ALU.pow).then_inc(done, 1)

            rsqrt(var1, rstd1, ln1_step, LN_STEPS, rstd1_done)

            def body(n, h, par, ff, old, att, nxt):
                m = n + 1
                for e in range(NE):
                    u, r = 9 * n + e, (par + e) % 2
                    if ff and e > 0 or old and e == 0:
                        pool.wait_ge(act_hi_ready, u)
                        pool.tensor_tensor(act_lo[1 - r][:], act[1 - r][:], act_hi[1 - r][:].bitcast(F32),
                                           ALU.subtract).then_inc(act_lo_ready, 1)
                    if att and e == 3:
                        if isinstance(n, int) and n == -1:
                            pool.wait_ge(c_loaded, 64)
                        if not (isinstance(m, int) and m < 1):
                            pool.wait_ge(y_ready, 4 * m)
                        pool.tensor_tensor(x_bo[:], x_sb[1 - par][:], row[:, 0:D].unsqueeze(1).to_broadcast([P, CH, D]),
                                           ALU.add).then_inc(xbo_ready, 1)
                    if att and e == 5:
                        rsqrt(var2, rstd2, ln2_step, LN_STEPS * (m + 1), rstd2_done)
                    if nxt and e == 7:
                        rsqrt(var1, rstd1, ln1_step, LN_STEPS * (m + 2), rstd1_done)
                    if ff and e >= 1:
                        pool.wait_ge(glu_ready, u + 1)
                        pool.wait_ge(cw_copied, NR * n + e)
                        pool.tensor_tensor(glu_w[r][:], glu[r][:], cw_wide[r][:], ALU.mult).then_inc(gluw_ready, 1)
                    if isinstance(n, int) and n == -1:
                        pool.wait_ge(w_hi_done, 2 * e + 2)
                        pool.tensor_tensor(up_lo[:, e], up_f32[:, e], up_hi[:, e].bitcast(F32), ALU.subtract).then_inc(w_lo_done, 1)
                        pool.tensor_tensor(down_lo[:, e], down_f32[:, e], down_hi[:, e].bitcast(F32), ALU.subtract).then_inc(w_lo_done, 1)

            walk(pool, body)

        @block.tensor
        def _(pe):
            def three(out_ap, w_hi, w_lo, x_hi, x_lo, start=True, stop=True):
                pe.matmul(out_ap, w_hi, x_hi, start=start, stop=False)
                pe.matmul(out_ap, w_hi, x_lo, start=False, stop=False)
                return pe.matmul(out_ap, w_lo, x_hi, start=False, stop=stop)

            def transposes(dst, src):
                for c in range(CH):
                    i = pe.transpose(dst[:, c * P:(c + 1) * P], src(c), ident[:])
                return i

            pe.wait_ge(aw_loaded, 16)
            pe.wait_ge(dve_const, 1)
            pe.matmul(at_bank[1][:, 0:D], attn_sb[:, 2], attn_sb[:, 3], start=True, stop=True)
            pe.matmul(at_bank[1][:, D:2 * D], bv_wide[:], attn_sb[:, 3], start=True, stop=True).then_inc(wov_mm, 1)

            def norm1_T(m):
                pe.wait_ge(xn_ready, m + 1)
                transposes(at_bank[0], lambda c: xn[:, c]).then_inc(t1_done, 1)

            pe.wait_ge(pool_const, 6)
            norm1_T(0)

            def down(n, par, e):
                pe.wait_ge(act_lo_ready, 9 * n + e + 1)
                if e == 0:
                    if not (isinstance(n, int) and n == 0):
                        pe.wait_ge(ff_copied, n)
                    pe.wait_ge(cwT_ready, n + 1)
                    pe.matmul(ff_bank[:], b2_hi[:], cwT[par][:], start=True, stop=False)
                    pe.matmul(ff_bank[:], b2_lo[:], cwT[par][:], start=False, stop=False)
                r = (par + e) % 2
                three(ff_bank[:], down_hi[:, e], down_lo[:, e], act_hi[r][:], act_lo[r][:],
                      start=False, stop=(e == NE - 1)).then_inc(down_done, 1)

            def body(n, h, par, ff, old, att, nxt):
                m = n + 1
                for e in range(NE):
                    u = 9 * n + e
                    first = isinstance(u, int) and u == 0
                    if ff:
                        if e == 0:
                            pe.wait_ge(ynT_hi_ready, n + 1)
                            pe.wait_ge(ynT_lo_ready, n + 1)
                        if isinstance(n, int) and n == 0:
                            pe.wait_ge(w_lo_done, 2 * e + 2)
                        for k in range(4):
                            if not first:
                                pe.wait_ge(h_used if k % 2 else h3_copied, 2 * u - 1 + k // 2)
                            three(h_bank[k][:], up_hi[:, e, k], up_lo[:, e, k], ynT_hi[par][:],
                                  ynT_lo[par][:]).then_inc(h_ready, 1)
                            if k == 1 and e >= 1:
                                if e == 1:
                                    pe.wait_ge(cwT_ready, n + 1)
                                if not (isinstance(n, int) and n == 0 and e == 1):
                                    pe.wait_ge(cw_copied, NR * n + e - 1)
                                if old and e == 3:
                                    pe.wait_ge(o_ready, n)
                                pe.matmul(cw_bank[:], pick[:, e - 1], cwT[par][:], start=True,
                                          stop=True).then_inc(cw_mm, 1)
                    if ff and e >= 2:
                        down(n, par, e - 2)
                    if old and e < 2:
                        down(n - 1, 1 - par, NE - 2 + e)
                    if ff and e == 0:
                        pe.wait_ge(cw_ready, n + 1)
                        if not (isinstance(n, int) and n == 0):
                            pe.wait_ge(cw_copied, NR * n)
                        for c in range(CH):
                            i = pe.transpose(cw_bank[0:2 * NR, c * P:(c + 1) * P], cw_parts[:, c].bitcast(F32), ident[:])
                        i.then_inc(cwT_mm, 1)
                    if old and e == 2:
                        pe.wait_ge(ff_copied, n)
                        if ff:
                            pe.wait_ge(cw_copied, NR * n + 2)
                        transposes(cw_bank, lambda c: ffT[:, c * P:(c + 1) * P]).then_inc(ffo_mm, 1)
                    if att and e == 0:
                        pe.wait_ge(xnT_ready, m + 1)
                        if isinstance(n, int) and n == -1:
                            pe.wait_ge(wov_ready, 2)
                        pe.matmul(at_bank[1][:], attn_sb[:, 0], xnT[:], start=True, stop=True).then_inc(q_mm, 1)
                        pe.matmul(at_bank[0][:], attn_sb[:, 1], xnT[:], start=True, stop=True).then_inc(k_mm, 1)
                    if att and e == 1:
                        pe.wait_ge(q_read, 2 * m + 2)
                        for c in range(CH):
                            i = pe.matmul(at_bank[1][:, c * D:(c + 1) * D], xnT[:, c * P:(c + 1) * P], wov[:],
                                          start=True, stop=True)
                        i.then_inc(v_mm, 1)
                    if att and e == 2:
                        pe.wait_ge(qk_ready, 2 * m + 2)
                        def scores(dst, s, t):
                            return pe.matmul(dst, kf[:, s * P:(s + 1) * P], qf[:, t * P:(t + 1) * P],
                                             start=True, stop=True)
                        for c in range(CH):
                            i = scores(at_bank[0][:, c * P:(c + 1) * P], c, c)
                        i.then_inc(diag_mm, 1)
                        pe.wait_ge(v_ready, m + 1)
                        for k in range(4):
                            i = scores(at_bank[1][:, k * P:(k + 1) * P], *OFF[k])
                        i.then_inc(off_mm, 1)
                    if att and e == 3:
                        pe.wait_ge(diag_ready, m + 1)
                        for k in range(2):
                            i = scores(at_bank[0][:, k * P:(k + 1) * P], *OFF[4 + k])
                        i.then_inc(off2_mm, 1)
                    if att and e == 4:
                        pe.wait_ge(off_ready, m + 1)
                        pe.wait_ge(off2_ready, m + 1)
                        for c in range(CH):
                            dst = at_bank[1 - c // 2][:, (c % 2) * (D + 1):(c % 2 + 1) * (D + 1)]
                            for s in range(c + 1):
                                w = a_diag[:, c] if s == c else a_off[:, OFF.index((s, c))]
                                i = pe.matmul(dst, w, v1[:, s], start=(s == 0), stop=(s == c))
                            if c % 2:
                                i.then_inc(num_mm, 1)
                    if att and e == 6:
                        pe.wait_ge(yn_ready, m + 1)
                        transposes(at_bank[1], lambda c: yn[:, c]).then_inc(t2_done, 1)
                    if att and e == 7:
                        pe.wait_ge(ynT_lo_ready, m + 1)
                        if isinstance(n, int) and n == -1:
                            pe.wait_ge(dve_const, 6)
                        for c in range(CH):
                            t = slice(c * P, (c + 1) * P)
                            i = three(at_bank[0][:, c * NR:(c + 1) * NR], ynT_hi[1 - par][:, t], ynT_lo[1 - par][:, t],
                                      gate_hi[:], gate_lo[:])
                        i.then_inc(gate_mm, 1)
                    if nxt and e == 8:
                        pe.wait_ge(lg_ready, m + 1)
                        norm1_T(m + 1)

            walk(pe, body)


def kernel(**inputs):
    import numpy as _np
    import concourse.bacc as _bacc
    from concourse import mybir as _mybir
    from concourse.bass_utils import run_bass_kernel_spmd as _run

    a = {k: _np.asarray(v) for k, v in inputs.items()}
    ffn, attn = "L0_ffn_", "L0_attn_"
    x = a[attn + "chunk"]

    def up(name):
        w = _np.concatenate([a[ffn + "s" + name][None], a[ffn + name]])
        return w.reshape(w.shape[0], -1, 2, w.shape[2]).transpose(3, 0, 2, 1)

    def up_bias(name):
        b = _np.concatenate([a[ffn + "s" + name][None], a[ffn + name]])
        return b.reshape(b.shape[0], -1, 2).transpose(1, 0, 2)

    w_up = _np.stack([up("w3"), up("w1")], axis=3).reshape(128, 9, 4, 128)
    b_up = _np.stack([up_bias("b3"), up_bias("b1")], axis=3).reshape(128, 36)
    w_down = _np.concatenate([a[ffn + "sw2"][None], a[ffn + "w2"]]).transpose(2, 0, 1)
    attn_w = _np.stack([a[attn + "Wq"].T, a[attn + "Wk"].T, a[attn + "Wv"], a[attn + "Wo"].T], axis=1)
    cols = _np.concatenate([b_up] + [a[k][:, None] for k in (attn + "bq", attn + "bk", attn + "bv", ffn + "sb2")], axis=1)
    rows = _np.broadcast_to(_np.concatenate([a[attn + "bo"], a[ffn + "gate_b"]])[None], (128, 136))
    arrays = {
        "in_x": x.reshape(-1, x.shape[-1]), "in_w_up": w_up, "in_w_down": w_down, "in_attn_w": attn_w,
        "in_cols": cols, "in_rows": rows, "in_gate_w": a[ffn + "gate_w"].T,
        "in_b2rows": _np.concatenate([a[ffn + "b2"], a[ffn + "b2"]]),
    }
    arrays = {k: _np.ascontiguousarray(v) for k, v in arrays.items()}
    nc = _bacc.Bacc("TRN2", target_bir_lowering=False, num_devices=1)
    args = [nc.dram_tensor(k, v.shape, _mybir.dt.from_np(v.dtype), kind="ExternalInput").ap()
            for k, v in arrays.items()]
    args.append(nc.dram_tensor("out", arrays["in_x"].shape, _mybir.dt.float32, kind="ExternalOutput").ap())
    block_kernel(nc, *args)
    r = _run(nc, [arrays], core_ids=[0])
    return r.results[0]["out"].reshape(x.shape)
```

```python
from contextlib import ExitStack

import concourse.bass as bass
from concourse import mybir

F32 = mybir.dt.float32
F32R = mybir.dt.float32r
ACT = mybir.ActivationFunctionType
ALU = mybir.AluOpType
AX_X = mybir.AxisListType.X

P = 128
D = 128
TOK = 512
CH = TOK // P
NR = 8
NE = NR + 1
LIMIT = 7.0
LN_EPS = 1e-5
DEN_EPS = 1e-6
ROUTE_STEPS = 17
LN_STEPS = 5
BIG = 1e30

C_BUP, C_BQ, C_BK, C_BV, C_SB2, N_COL = 0, 4 * NE, 4 * NE + 1, 4 * NE + 2, 4 * NE + 3, 4 * NE + 4


def block_kernel(nc, x_in, w_up, w_down, attn_w, cols, rows, gate_w, b2rows, out):
    NB = x_in.shape[0] // TOK
    x_b = x_in.rearrange("(b c p) d -> b p c d", c=CH, p=P)
    out_b = out.rearrange("(b c p) d -> b p c d", c=CH, p=P)

    cw_dram = nc.dram_tensor("cw_dram", [2, NR, TOK], F32, kind="Internal").ap()

    with ExitStack() as ctx:
        def sb(name, shape, dt=F32):
            return ctx.enter_context(nc.sbuf_tensor(name, shape, dt))

        def bank(name):
            return ctx.enter_context(nc.psum_tensor(name, [P, TOK], F32))

        def sem(name):
            return ctx.enter_context(nc.semaphore(name))

        up_f32 = sb("up_f32", [P, NE, 4, P])
        down_f32 = sb("down_f32", [P, NE, D])
        up_hi, up_lo = sb("up_hi", [P, NE, 4, P], F32R), sb("up_lo", [P, NE, 4, P], F32R)
        down_hi, down_lo = sb("down_hi", [P, NE, D], F32R), sb("down_lo", [P, NE, D], F32R)
        attn_sb = sb("attn_sb", [P, 4, P])
        wov = sb("wov", [P, D])
        bvo = sb("bvo", [P, D])
        bv_wide = sb("bv_wide", [P, P])
        col = sb("col", [P, N_COL])
        row = sb("row", [P, D + NR])
        gate_f32 = sb("gate_f32", [P, NR])
        gate_hi, gate_lo = sb("gate_hi", [P, NR], F32R), sb("gate_lo", [P, NR], F32R)
        b2_sb = sb("b2_sb", [NR, D])
        ident = sb("ident", [P, P])
        causal = sb("causal", [P, P])
        rank = sb("rank", [P, NR])
        minus_half = sb("minus_half", [P, CH])

        x_sb = [sb(f"x_sb{i}", [P, CH, D]) for i in range(2)]
        stats1, mv1 = sb("stats1", [P, CH, 6]), sb("mv1", [P, 6, CH])
        stats2, mv2 = sb("stats2", [P, CH, 6]), sb("mv2", [P, 6, CH])
        var1, rstd1 = sb("var1", [P, CH]), sb("rstd1", [P, CH])
        var2, rstd2 = sb("var2", [P, CH]), sb("rstd2", [P, CH])
        xn = sb("xn", [P, CH, D])
        xnT = sb("xnT", [P, TOK])
        q_exp, q_relu, qf = sb("q_exp", [P, TOK]), sb("q_relu", [P, TOK]), sb("qf", [P, TOK])
        k_exp, k_relu, kf = sb("k_exp", [P, TOK]), sb("k_relu", [P, TOK]), sb("kf", [P, TOK])
        v1 = sb("v1", [P, CH, D + 1])
        a_diag = sb("a_diag", [P, CH, P])
        a_off = sb("a_off", [P, 6, P])
        x_bo = sb("x_bo", [P, CH, D])
        den, rden = sb("den", [P, CH]), sb("rden", [P, CH])
        y_sb = [sb(f"y_sb{i}", [P, CH, D]) for i in range(2)]
        yn = sb("yn", [P, CH, D])
        ynT_hi = [sb(f"ynT_hi{i}", [P, TOK], F32R) for i in range(2)]
        ynT_lo = [sb(f"ynT_lo{i}", [P, TOK], F32R) for i in range(2)]

        r_max, r_lg, r_ex = sb("r_max", [P, CH]), sb("r_lg", [P, CH, NR]), sb("r_ex", [P, CH, NR])
        r_sum, r_inv, r_sc = sb("r_sum", [P, CH]), sb("r_inv", [P, CH]), sb("r_sc", [P, CH, NR])
        r_b, r_m = sb("r_b", [P, CH, NR]), sb("r_m", [P, 2, CH])
        r_eq, r_w = sb("r_eq", [P, 2, CH, NR]), sb("r_w", [P, 2, CH, NR])
        r_f, r_oh = sb("r_f", [P, 2, CH]), sb("r_oh", [P, 2, CH, NR])
        r_b2, r_sel, r_cw = sb("r_b2", [P, CH, NR]), sb("r_sel", [P, CH, NR]), sb("r_cw", [P, CH, NR])
        cwT = [sb(f"cwT{i}", [NR, TOK]) for i in range(2)]
        cw_wide = sb("cw_wide", [P, NR, TOK])

        h3_sb = [[sb(f"h3_sb{i}{h}", [P, TOK]) for h in "gl"] for i in range(2)]
        gate_act = [sb(f"gate_act{i}", [P, TOK]) for i in range(2)]
        lin = [sb(f"lin{i}", [P, TOK]) for i in range(2)]
        glu = [sb(f"glu{i}", [P, TOK]) for i in range(2)]
        glu_w = [sb(f"glu_w{i}", [P, TOK]) for i in range(2)]
        act = [sb(f"act{i}", [P, TOK]) for i in range(2)]
        act_hi = [sb(f"act_hi{i}", [P, TOK], F32R) for i in range(2)]
        act_lo = [sb(f"act_lo{i}", [P, TOK], F32R) for i in range(2)]
        ffT = sb("ffT", [P, TOK])
        o_sb = [sb(f"o_sb{i}", [P, CH, D]) for i in range(2)]

        h_bank = [bank(f"h_bank{k}") for k in range(4)]
        ff_bank = bank("ff_bank")
        misc_bank = bank("misc_bank")
        at_bank = [bank(f"at_bank{k}") for k in range(2)]

        w_loaded = [sem(f"w_loaded{e}") for e in range(NE)]
        c_loaded, aw_loaded = sem("c_loaded"), sem("aw_loaded")
        x_loaded = [sem("x_loaded0"), sem("x_loaded1")]
        o_stored = [sem("o_stored0"), sem("o_stored1")]
        pool_const, dve_const = sem("pool_const"), sem("dve_const")
        w_hi_done, w_lo_done = sem("w_hi_done"), sem("w_lo_done")
        wov_mm, wov_ready = sem("wov_mm"), sem("wov_ready")
        ln1_step, ln2_step, route_step, den_step = (sem("ln1_step"), sem("ln2_step"),
                                                    sem("route_step"), sem("den_step"))
        rstd1_done, rstd2_done = sem("rstd1_done"), sem("rstd2_done")
        xn_ready, t1_done, xnT_ready = sem("xn_ready"), sem("t1_done"), sem("xnT_ready")
        q_mm, k_mm, v_mm = sem("q_mm"), sem("k_mm"), sem("v_mm")
        q_read, k_read = sem("q_read"), sem("k_read")
        qk_ready, v_ready = sem("qk_ready"), sem("v_ready")
        diag_mm, off_mm, off2_mm = sem("diag_mm"), sem("off_mm"), sem("off2_mm")
        diag_ready, off_ready, off2_ready = sem("diag_ready"), sem("off_ready"), sem("off2_ready")
        xbo_ready, num_mm, y_ready = sem("xbo_ready"), sem("num_mm"), sem("y_ready")
        yn_ready, t2_done = sem("yn_ready"), sem("t2_done")
        ynT_hi_ready, ynT_lo_ready = sem("ynT_hi_ready"), sem("ynT_lo_ready")
        gate_mm, lg_ready, ex_ready = sem("gate_mm"), sem("lg_ready"), sem("ex_ready")
        cw_ready, cwT_mm, cwT_ready = sem("cw_ready"), sem("cwT_mm"), sem("cwT_ready")
        h_ready, h3_copied, h_used = sem("h_ready"), sem("h3_copied"), sem("h_used")
        ga_ready, lin_ready, glu_ready = sem("ga_ready"), sem("lin_ready"), sem("glu_ready")
        cw_written, gluw_ready = sem("cw_written"), sem("gluw_ready")
        cw_loaded = [sem(f"cw_loaded{e}") for e in range(NR)]
        act_ready, act_hi_ready, act_lo_ready = sem("act_ready"), sem("act_hi_ready"), sem("act_lo_ready")
        down_done, ff_copied = sem("down_done"), sem("ff_copied")
        ffo_mm, o_ready = sem("ffo_mm"), sem("o_ready")

        OFF = [(0, 1), (0, 2), (0, 3), (2, 3), (1, 2), (1, 3)]

        def walk(eng, body):
            body(-2, -1, 0, False, False, False, True)
            body(-1, -1, 1, False, False, True, True)
            body(0, 0, 0, True, False, True, True)
            with eng.Fori(0, (NB - 4) // 2) as i:
                body(2 * i + 1, i, 1, True, True, True, True)
                body(2 * i + 2, i + 1, 0, True, True, True, True)
            body(NB - 3, (NB - 3) // 2, 1, True, True, True, True)
            body(NB - 2, (NB - 2) // 2, 0, True, True, True, False)
            body(NB - 1, (NB - 1) // 2, 1, True, True, False, False)
            body(NB, NB // 2, 0, False, True, False, False)

        block = ctx.enter_context(nc.Block())

        @block.sync
        def _(sp):
            sp.dma_start(x_sb[0][:], x_b[0]).then_inc(x_loaded[0], 16)
            sp.dma_start(col[:], cols).then_inc(c_loaded, 16)
            sp.dma_start(attn_sb[:], attn_w).then_inc(aw_loaded, 16)
            sp.dma_start(row[:], rows).then_inc(c_loaded, 16)
            sp.dma_start(gate_f32[:], gate_w).then_inc(c_loaded, 16)
            sp.dma_start(b2_sb[:], b2rows).then_inc(c_loaded, 16)
            sp.dma_start(x_sb[1][:], x_b[1]).then_inc(x_loaded[1], 16)
            for e in range(NE):
                sp.dma_start(up_f32[:, e], w_up[:, e]).then_inc(w_loaded[e], 16)
                sp.dma_start(down_f32[:, e], w_down[:, e]).then_inc(w_loaded[e], 16)

            def body(n, h, par, ff, old, late, early):
                if ff:
                    sp.wait_ge(cwT_ready, n + 1)
                    sp.dma_start(cw_dram[par], cwT[par][:]).then_inc(cw_written, 16)
                    sp.wait_ge(cw_written, 16 * n + 16)
                    for e in range(NR):
                        if not (isinstance(n, int) and n == 0):
                            sp.wait_ge(gluw_ready, NR * n - NR + e + 1)
                        sp.dma_start(cw_wide[:, e], cw_dram[par, e:e + 1].broadcast_to([P, TOK])).then_inc(cw_loaded[e], 16)
                if early and not (isinstance(n, int) and (n < -1 or n + 3 >= NB)):
                    sp.wait_ge(xbo_ready, n + 2)
                    sp.dma_start(x_sb[1 - par][:], x_b[n + 3]).then_inc(x_loaded[1 - par], 16)
                if old:
                    sp.wait_ge(o_ready, n)
                    sp.dma_start(out_b[n - 1], o_sb[1 - par][:]).then_inc(o_stored[1 - par], 16)

            walk(sp, body)
            for i in range(2):
                sp.wait_ge(o_stored[i], 16 * (NB // 2))

        @block.scalar
        def _(act_e):
            def split_hi(e):
                act_e.wait_ge(w_loaded[e], 32)
                act_e.activation(up_hi[:, e], up_f32[:, e], ACT.Copy).then_inc(w_hi_done, 1)
                act_e.activation(down_hi[:, e], down_f32[:, e], ACT.Copy).then_inc(w_hi_done, 1)

            act_e.wait_ge(wov_mm, 1)
            act_e.activation(wov[:], at_bank[1][:, 0:D], ACT.Copy).then_inc(wov_ready, 1)
            act_e.activation(bvo[:], at_bank[1][:, D:2 * D], ACT.Copy).then_inc(wov_ready, 1)

            def body(n, h, par, ff, old, late, early):
                m = n + 1
                for e in range(NE):
                    u, r = 9 * n + e, (par + e) % 2
                    if ff:
                        act_e.wait_ge(h_ready, 4 * u + 1)
                        act_e.activation(h3_sb[r][0][:], h_bank[0][:], ACT.Identity,
                                         bias=col[:, 4 * e:4 * e + 1]).then_inc(h3_copied, 1)
                    if ff and e == 0:
                        act_e.wait_ge(cwT_mm, n + 1)
                        act_e.activation(cwT[par][:], misc_bank[0:NR, :], ACT.Copy).then_inc(cwT_ready, 1)
                    if late and e == 1:
                        act_e.wait_ge(off_mm, m + 1)
                        act_e.activation(a_off[:, 0:4], at_bank[1][:].rearrange("p (k t) -> p k t", t=P),
                                         ACT.Copy).then_inc(off_ready, 1)
                    if late and e == 2:
                        act_e.wait_ge(off2_mm, m + 1)
                        act_e.activation(a_off[:, 4:6], at_bank[0][:, 0:2 * P].rearrange("p (k t) -> p k t", t=P),
                                         ACT.Copy).then_inc(off2_ready, 1)
                    if old and e == 2:
                        act_e.wait_ge(down_done, NE * n)
                        act_e.activation(ffT[:], ff_bank[:], ACT.Identity,
                                         bias=col[:, C_SB2:C_SB2 + 1]).then_inc(ff_copied, 1)
                    if late and e == 5:
                        act_e.wait_ge(t2_done, m + 1)
                        act_e.activation(ynT_hi[1 - par][:], at_bank[1][:], ACT.Copy).then_inc(ynT_hi_ready, 1)
                    if early and e == 5:
                        act_e.wait_ge(t1_done, m + 2)
                        act_e.activation(xnT[:], at_bank[0][:], ACT.Copy).then_inc(xnT_ready, 1)
                    if ff and e > 0 or old and e == 0:
                        act_e.wait_ge(act_ready, u)
                        if not (isinstance(u, int) and u < 3):
                            act_e.wait_ge(down_done, u - 2)
                        act_e.activation(act_hi[1 - r][:], act[1 - r][:], ACT.Copy).then_inc(act_hi_ready, 1)
                    if ff:
                        act_e.wait_ge(h_ready, 4 * u + 3)
                        act_e.activation(h3_sb[r][1][:], h_bank[2][:], ACT.Identity,
                                         bias=col[:, 4 * e + 2:4 * e + 3]).then_inc(h3_copied, 1)
                        act_e.wait_ge(ga_ready, u + 1)
                        act_e.activation(glu[r][:], gate_act[r][:],
                                         ACT.Gelu_apprx_sigmoid).then_inc(glu_ready, 1)
                    if late and e == 6:
                        act_e.wait_ge(lg_ready, m + 1)
                        act_e.activation(r_ex[:], r_lg[:], ACT.Exp).then_inc(ex_ready, 1)
                    if early and e == 6:
                        act_e.wait_ge(q_mm, m + 2)
                        act_e.activation(q_exp[:], at_bank[1][:], ACT.Exp,
                                         bias=col[:, C_BQ:C_BQ + 1]).then_inc(q_read, 1)
                        act_e.wait_ge(k_mm, m + 2)
                        act_e.activation(k_exp[:], at_bank[0][:], ACT.Exp,
                                         bias=col[:, C_BK:C_BK + 1]).then_inc(k_read, 1)
                        act_e.activation(q_relu[:], at_bank[1][:], ACT.Relu,
                                         bias=col[:, C_BQ:C_BQ + 1]).then_inc(q_read, 1)
                        act_e.activation(k_relu[:], at_bank[0][:], ACT.Relu,
                                         bias=col[:, C_BK:C_BK + 1]).then_inc(k_read, 1)
                    if isinstance(n, int) and n == -1:
                        split_hi(e)

            walk(act_e, body)

        @block.vector
        def _(dve):
            def chunk_bc(small):
                return small.unsqueeze(2).to_broadcast([P, CH, NR])

            def norm_stats(src, stats, mv, var, step, m, x_wait=None):
                if x_wait is not None:
                    dve.wait_ge(*x_wait)
                for c in range(CH):
                    i = dve.bn_stats(stats[:, c], src[:, c])
                i.then_inc(step, 1)
                dve.wait_ge(step, LN_STEPS * m + 1)
                dve.tensor_tensor(mv[:, 0], stats[:, :, 1], stats[:, :, 4], ALU.add)
                dve.tensor_tensor(mv[:, 1], stats[:, :, 1], stats[:, :, 4], ALU.subtract)
                dve.tensor_tensor(mv[:, 2], stats[:, :, 2], stats[:, :, 5], ALU.add).then_inc(step, 1)
                dve.wait_ge(step, LN_STEPS * m + 2)
                dve.tensor_scalar(mv[:, 3], mv[:, 0], 0.5, None, ALU.mult)
                dve.scalar_tensor_tensor(mv[:, 4], mv[:, 1], 0.25, mv[:, 1], ALU.mult, ALU.mult).then_inc(step, 1)
                dve.wait_ge(step, LN_STEPS * m + 3)
                dve.tensor_scalar(mv[:, 5], mv[:, 4], LN_EPS, None, ALU.add).then_inc(step, 1)
                dve.wait_ge(step, LN_STEPS * m + 4)
                dve.scalar_tensor_tensor(var[:], mv[:, 2], 1.0 / D, mv[:, 5], ALU.mult, ALU.add).then_inc(step, 1)

            def normalize(dst, src, mv, rstd, ready):
                for c in range(CH):
                    i = dve.tensor_scalar(dst[:, c], src[:, c], mv[:, 3, c:c + 1], rstd[:, c:c + 1],
                                          ALU.subtract, ALU.mult)
                i.then_inc(ready, 1)

            dve.wait_ge(c_loaded, 64)
            dve.tensor_copy(bv_wide[:], col[:, C_BV:C_BV + 1].to_broadcast([P, P])).then_inc(dve_const, 1)
            dve.tensor_copy(gate_hi[:], gate_f32[:]).then_inc(dve_const, 1)
            dve.wait_ge(dve_const, 2)
            dve.tensor_tensor(gate_lo[:], gate_f32[:], gate_hi[:].bitcast(F32), ALU.subtract).then_inc(dve_const, 1)
            dve.wait_ge(pool_const, 7)

            def routing_scores(m):
                dve.wait_ge(gate_mm, m + 1)
                lg = misc_bank[:, 0:CH * NR].rearrange("p (c r) -> p c r", r=NR)
                dve.reduce_max(r_max[:], lg, AX_X).then_inc(route_step, 1)
                dve.wait_ge(route_step, ROUTE_STEPS * m + 1)
                dve.tensor_tensor(r_lg[:], lg, chunk_bc(r_max[:]), ALU.subtract).then_inc(lg_ready, 1)

            def routing_choice(m, second):
                step = [10 if second else 1]

                def link(ins):
                    step[0] += 1
                    ins.then_inc(route_step, 1)
                    dve.wait_ge(route_step, ROUTE_STEPS * m + step[0])

                def best(k, src):
                    link(dve.reduce_max(r_m[:, k], src[:], AX_X))
                    link(dve.tensor_tensor(r_eq[:, k], src[:], chunk_bc(r_m[:, k]), ALU.is_equal))
                    link(dve.tensor_tensor(r_w[:, k], r_eq[:, k], rank[:].unsqueeze(1).to_broadcast([P, CH, NR]), ALU.mult))
                    link(dve.reduce_max(r_f[:, k], r_w[:, k], AX_X))
                    link(dve.tensor_tensor(r_oh[:, k], r_w[:, k], chunk_bc(r_f[:, k]), ALU.is_equal))

                if not second:
                    dve.wait_ge(ex_ready, m + 1)
                    link(dve.reduce_sum(r_sum[:], r_ex[:], AX_X))
                    link(dve.reciprocal(r_inv[:], r_sum[:]))
                    link(dve.tensor_tensor(r_sc[:], r_ex[:], chunk_bc(r_inv[:]), ALU.mult))
                    link(dve.tensor_tensor(r_b[:], r_sc[:], row[:, D:D + NR].unsqueeze(1).to_broadcast([P, CH, NR]), ALU.add))
                    best(0, r_b)
                    assert step[0] == 10
                else:
                    link(dve.scalar_tensor_tensor(r_b2[:], r_oh[:, 0], -BIG, r_b[:], ALU.mult, ALU.add))
                    best(1, r_b2)
                    link(dve.tensor_tensor(r_sel[:], r_oh[:, 0], r_oh[:, 1], ALU.add))
                    assert step[0] == ROUTE_STEPS
                    dve.tensor_tensor(r_cw[:], r_sel[:], r_sc[:], ALU.mult).then_inc(cw_ready, 1)

            def body(n, h, par, ff, old, late, early):
                m = n + 1
                for e in range(NE):
                    u, r = 9 * n + e, (par + e) % 2
                    if late and e == 1:
                        dve.wait_ge(diag_mm, m + 1)
                        dve.tensor_tensor(a_diag[:], at_bank[0][:].rearrange("p (c t) -> p c t", t=P),
                                          causal[:].unsqueeze(1).to_broadcast([P, CH, P]), ALU.mult).then_inc(diag_ready, 1)
                    if old and e == 3:
                        dve.wait_ge(ffo_mm, n)
                        if not (isinstance(n, int) and n < 3):
                            dve.wait_ge(o_stored[1 - par], 16 * (h - (1 if par == 0 else 0)))
                        dve.tensor_tensor(o_sb[1 - par][:], misc_bank[:].rearrange("p (c d) -> p c d", d=D),
                                          y_sb[1 - par][:], ALU.add).then_inc(o_ready, 1)
                    if late and e == 3:
                        dve.wait_ge(xbo_ready, m + 1)
                        for g in range(2):
                            o = at_bank[1 - g][:, 0:2 * (D + 1)].rearrange("p (c d) -> p c d", d=D + 1)
                            dve.wait_ge(num_mm, 2 * m + g + 1)
                            dve.tensor_scalar(den[:, 2 * g:2 * g + 2], o[:, :, D], DEN_EPS, None, ALU.add).then_inc(den_step, 1)
                            dve.wait_ge(den_step, 4 * m + 2 * g + 1)
                            dve.reciprocal(rden[:, 2 * g:2 * g + 2], den[:, 2 * g:2 * g + 2]).then_inc(den_step, 1)
                            dve.wait_ge(den_step, 4 * m + 2 * g + 2)
                            for c in range(2):
                                dve.scalar_tensor_tensor(y_sb[1 - par][:, 2 * g + c], o[:, c, 0:D],
                                                         rden[:, 2 * g + c:2 * g + c + 1], x_bo[:, 2 * g + c],
                                                         ALU.mult, ALU.add).then_inc(y_ready, 1)
                    if late and e == 4:
                        dve.wait_ge(rstd2_done, m + 1)
                        normalize(yn, y_sb[1 - par], mv2, rstd2, yn_ready)
                    if early and e == 2:
                        dve.wait_ge(rstd1_done, m + 2)
                        normalize(xn, x_sb[par], mv1, rstd1, xn_ready)
                    if late and e == 5:
                        dve.wait_ge(t2_done, m + 1)
                        dve.wait_ge(ynT_hi_ready, m + 1)
                        dve.tensor_tensor(ynT_lo[1 - par][:], at_bank[1][:], ynT_hi[1 - par][:].bitcast(F32),
                                          ALU.subtract).then_inc(ynT_lo_ready, 1)
                    if early and e == 7:
                        dve.wait_ge(q_read, 2 * m + 4)
                        dve.scalar_tensor_tensor(qf[:], q_exp[:], 1.0, q_relu[:], ALU.min, ALU.add).then_inc(qk_ready, 1)
                        dve.wait_ge(k_read, 2 * m + 4)
                        dve.scalar_tensor_tensor(kf[:], k_exp[:], 1.0, k_relu[:], ALU.min, ALU.add).then_inc(qk_ready, 1)
                    if late and e == 6:
                        routing_scores(m)
                    if early and e == 8:
                        dve.wait_ge(v_mm, m + 2)
                        dve.tensor_tensor(v1[:, :, 0:D], at_bank[1][:].rearrange("p (c d) -> p c d", d=D),
                                          bvo[:].unsqueeze(1).to_broadcast([P, CH, D]), ALU.add).then_inc(v_ready, 1)
                    if ff:
                        dve.wait_ge(h3_copied, 2 * u + 1)
                        dve.wait_ge(h_ready, 4 * u + 2)
                        dve.scalar_tensor_tensor(gate_act[r][:], h_bank[1][:], col[:, 4 * e + 1:4 * e + 2],
                                                 h3_sb[r][0][:], ALU.add, ALU.mult).then_inc(h_used, 1)
                    if ff and e > 0 or old and e == 0:
                        dve.wait_ge(lin_ready, u)
                        if e == 1:
                            dve.wait_ge(glu_ready, u)
                            if not (isinstance(u, int) and u < 3):
                                dve.wait_ge(act_lo_ready, u - 2)
                            src = glu
                        else:
                            dve.wait_ge(gluw_ready, NR * n + (e - 1 if e else 0))
                            src = glu_w
                        dve.scalar_tensor_tensor(act[1 - r][:], lin[1 - r][:], 1.0, src[1 - r][:],
                                                 ALU.add, ALU.mult).then_inc(act_ready, 1)
                    if ff:
                        dve.wait_ge(h_used, 2 * u + 1)
                        dve.tensor_scalar(gate_act[r][:], gate_act[r][:], LIMIT, None, ALU.min).then_inc(ga_ready, 1)
                        dve.wait_ge(h3_copied, 2 * u + 2)
                        dve.wait_ge(h_ready, 4 * u + 4)
                        dve.scalar_tensor_tensor(lin[r][:], h_bank[3][:], col[:, 4 * e + 3:4 * e + 4],
                                                 h3_sb[r][1][:], ALU.add, ALU.mult).then_inc(h_used, 1)
                    if late and e == 3:
                        norm_stats(y_sb[1 - par], stats2, mv2, var2, ln2_step, m, (y_ready, 4 * m + 4))
                    if early and e == 1:
                        norm_stats(x_sb[par], stats1, mv1, var1, ln1_step, m + 1, (x_loaded[par], 16 * (h + 2)))
                    if late and e == 7:
                        routing_choice(m, False)
                    if late and e == 8:
                        routing_choice(m, True)
                    if ff:
                        dve.wait_ge(h_used, 2 * u + 2)
                        dve.tensor_scalar(lin[r][:], lin[r][:], LIMIT, -LIMIT, ALU.min, ALU.max).then_inc(lin_ready, 1)

            walk(dve, body)

        @block.gpsimd
        def _(pool):
            def ones_where_zero(t, base, pattern, chan, count):
                pool.wait_ge(pool_const, count)
                pool.affine_select(out=t, in_=t, compare_op=ALU.not_equal, fill=1.0, base=base,
                                   pattern=pattern, channel_multiplier=chan).then_inc(pool_const, 1)

            pool.memset(minus_half[:], -0.5).then_inc(pool_const, 1)
            pool.memset(ident[:], 0.0).then_inc(pool_const, 1)
            pool.memset(causal[:], 1.0).then_inc(pool_const, 1)
            pool.memset(v1[:], 1.0).then_inc(pool_const, 1)
            ones_where_zero(ident[:], 0, [[-1, P]], 1, 2)
            pool.iota(rank[:], pattern=[[-1, NR]], base=NR, channel_multiplier=0,
                      allow_small_or_imprecise_dtypes=True).then_inc(pool_const, 1)
            pool.wait_ge(pool_const, 3)
            pool.affine_select(out=causal[:], in_=causal[:], compare_op=ALU.is_ge, fill=0.0, base=0,
                               pattern=[[1, P]], channel_multiplier=-1).then_inc(pool_const, 1)

            def rsqrt(var, rstd, step, count, done):
                pool.wait_ge(step, count)
                pool.tensor_tensor(rstd[:], var[:], minus_half[:], ALU.pow).then_inc(done, 1)

            def body(n, h, par, ff, old, late, early):
                m = n + 1
                for e in range(NE):
                    u, r = 9 * n + e, (par + e) % 2
                    if ff and e > 0 or old and e == 0:
                        pool.wait_ge(act_hi_ready, u)
                        pool.tensor_tensor(act_lo[1 - r][:], act[1 - r][:], act_hi[1 - r][:].bitcast(F32),
                                           ALU.subtract).then_inc(act_lo_ready, 1)
                    if late and e == 2:
                        if isinstance(n, int) and n == -1:
                            pool.wait_ge(c_loaded, 64)
                        if not (isinstance(m, int) and m < 1):
                            pool.wait_ge(y_ready, 4 * m)
                        pool.tensor_tensor(x_bo[:], x_sb[1 - par][:], row[:, 0:D].unsqueeze(1).to_broadcast([P, CH, D]),
                                           ALU.add).then_inc(xbo_ready, 1)
                    if ff and e >= 1:
                        pool.wait_ge(glu_ready, u + 1)
                        pool.wait_ge(cw_loaded[e - 1], 16 * n + 16)
                        pool.tensor_tensor(glu_w[r][:], glu[r][:], cw_wide[:, e - 1], ALU.mult).then_inc(gluw_ready, 1)
                    if late and e == 3:
                        rsqrt(var2, rstd2, ln2_step, LN_STEPS * (m + 1), rstd2_done)
                    if early and e == 1:
                        rsqrt(var1, rstd1, ln1_step, LN_STEPS * (m + 2), rstd1_done)
                    if isinstance(n, int) and n == -1:
                        pool.wait_ge(w_hi_done, 2 * e + 2)
                        pool.tensor_tensor(up_lo[:, e], up_f32[:, e], up_hi[:, e].bitcast(F32), ALU.subtract).then_inc(w_lo_done, 1)
                        pool.tensor_tensor(down_lo[:, e], down_f32[:, e], down_hi[:, e].bitcast(F32), ALU.subtract).then_inc(w_lo_done, 1)

            walk(pool, body)

        @block.tensor
        def _(pe):
            def three(out_ap, w_hi, w_lo, x_hi, x_lo, start=True, stop=True):
                pe.matmul(out_ap, w_hi, x_hi, start=start, stop=False)
                pe.matmul(out_ap, w_hi, x_lo, start=False, stop=False)
                return pe.matmul(out_ap, w_lo, x_hi, start=False, stop=stop)

            def transposes(dst, src):
                for c in range(CH):
                    i = pe.transpose(dst[:, c * P:(c + 1) * P], src(c), ident[:])
                return i

            pe.wait_ge(aw_loaded, 16)
            pe.wait_ge(dve_const, 1)
            pe.matmul(at_bank[1][:, 0:D], attn_sb[:, 2], attn_sb[:, 3], start=True, stop=True)
            pe.matmul(at_bank[1][:, D:2 * D], bv_wide[:], attn_sb[:, 3], start=True, stop=True).then_inc(wov_mm, 1)

            def scores(dst, s, t):
                return pe.matmul(dst, kf[:, s * P:(s + 1) * P], qf[:, t * P:(t + 1) * P], start=True, stop=True)

            pe.wait_ge(pool_const, 5)

            def down(n, par, e):
                pe.wait_ge(act_lo_ready, 9 * n + e + 1)
                if e == 0:
                    if not (isinstance(n, int) and n == 0):
                        pe.wait_ge(ff_copied, n)
                    pe.wait_ge(cwT_ready, n + 1)
                    pe.matmul(ff_bank[:], b2_sb[:], cwT[par][:], start=True, stop=False)
                r = (par + e) % 2
                three(ff_bank[:], down_hi[:, e], down_lo[:, e], act_hi[r][:], act_lo[r][:],
                      start=False, stop=(e == NE - 1)).then_inc(down_done, 1)

            def batch_rows(n):
                pe.wait_ge(ff_copied, n)
                transposes(misc_bank, lambda c: ffT[:, c * P:(c + 1) * P]).then_inc(ffo_mm, 1)

            def logits(n, par):
                pe.wait_ge(ynT_lo_ready, n + 2)
                if isinstance(n, int) and n == -1:
                    pe.wait_ge(dve_const, 3)
                elif not (isinstance(n, int) and n == 0):
                    pe.wait_ge(o_ready, n)
                for c in range(CH):
                    t = slice(c * P, (c + 1) * P)
                    i = three(misc_bank[:, c * NR:(c + 1) * NR], ynT_hi[1 - par][:, t], ynT_lo[1 - par][:, t],
                              gate_hi[:], gate_lo[:])
                i.then_inc(gate_mm, 1)

            def body(n, h, par, ff, old, late, early):
                m = n + 1
                for e in range(NE):
                    u = 9 * n + e
                    first = isinstance(u, int) and u == 0
                    if ff:
                        if e == 0:
                            pe.wait_ge(ynT_hi_ready, n + 1)
                            pe.wait_ge(ynT_lo_ready, n + 1)
                        if isinstance(n, int) and n == 0:
                            pe.wait_ge(w_lo_done, 2 * e + 2)
                        for k in range(4):
                            if not first:
                                pe.wait_ge(h_used if k % 2 else h3_copied, 2 * u - 1 + k // 2)
                            three(h_bank[k][:], up_hi[:, e, k], up_lo[:, e, k], ynT_hi[par][:],
                                  ynT_lo[par][:]).then_inc(h_ready, 1)
                    if ff and e >= 2:
                        down(n, par, e - 2)
                    if old and e < 2:
                        down(n - 1, 1 - par, NE - 2 + e)
                    if late and e == 0:
                        pe.wait_ge(qk_ready, 2 * m + 2)
                        for c in range(CH):
                            i = scores(at_bank[0][:, c * P:(c + 1) * P], c, c)
                        i.then_inc(diag_mm, 1)
                        pe.wait_ge(v_ready, m + 1)
                        for k in range(4):
                            i = scores(at_bank[1][:, k * P:(k + 1) * P], *OFF[k])
                        i.then_inc(off_mm, 1)
                    if late and e == 1:
                        pe.wait_ge(diag_ready, m + 1)
                        for k in range(2):
                            i = scores(at_bank[0][:, k * P:(k + 1) * P], *OFF[4 + k])
                        i.then_inc(off2_mm, 1)
                    if late and e == 2:
                        pe.wait_ge(off_ready, m + 1)
                        pe.wait_ge(off2_ready, m + 1)
                        for c in range(CH):
                            dst = at_bank[1 - c // 2][:, (c % 2) * (D + 1):(c % 2 + 1) * (D + 1)]
                            for s in range(c + 1):
                                w = a_diag[:, c] if s == c else a_off[:, OFF.index((s, c))]
                                i = pe.matmul(dst, w, v1[:, s], start=(s == 0), stop=(s == c))
                            if c % 2:
                                i.then_inc(num_mm, 1)
                    if old and e == 2:
                        batch_rows(n)
                    if late and e == 5:
                        logits(n, par)
                    if late and e == 8:
                        pe.wait_ge(cw_ready, n + 2)
                        for c in range(CH):
                            i = pe.transpose(misc_bank[0:NR, c * P:(c + 1) * P], r_cw[:, c], ident[:])
                        i.then_inc(cwT_mm, 1)
                    if late and e == 4:
                        pe.wait_ge(yn_ready, m + 1)
                        transposes(at_bank[1], lambda c: yn[:, c]).then_inc(t2_done, 1)
                    if early and e == 4:
                        if late:
                            pe.wait_ge(y_ready, 4 * m + 4)
                        pe.wait_ge(xn_ready, m + 2)
                        transposes(at_bank[0], lambda c: xn[:, c]).then_inc(t1_done, 1)
                    if early and e == 5:
                        pe.wait_ge(xnT_ready, m + 2)
                        if late:
                            pe.wait_ge(ynT_lo_ready, m + 1)
                        if isinstance(n, int) and n == -2:
                            pe.wait_ge(wov_ready, 2)
                        pe.matmul(at_bank[1][:], attn_sb[:, 0], xnT[:], start=True, stop=True).then_inc(q_mm, 1)
                        pe.matmul(at_bank[0][:], attn_sb[:, 1], xnT[:], start=True, stop=True).then_inc(k_mm, 1)
                    if early and e == 7:
                        pe.wait_ge(q_read, 2 * m + 4)
                        for c in range(CH):
                            i = pe.matmul(at_bank[1][:, c * D:(c + 1) * D], xnT[:, c * P:(c + 1) * P], wov[:],
                                          start=True, stop=True)
                        i.then_inc(v_mm, 1)

            walk(pe, body)


def kernel(**inputs):
    import numpy as _np
    import concourse.bacc as _bacc
    from concourse import mybir as _mybir
    from concourse.bass_utils import run_bass_kernel_spmd as _run

    a = {k: _np.asarray(v) for k, v in inputs.items()}
    ffn, attn = "L0_ffn_", "L0_attn_"
    x = a[attn + "chunk"]

    def up(name):
        w = _np.concatenate([a[ffn + "s" + name][None], a[ffn + name]])
        return w.reshape(w.shape[0], -1, 2, w.shape[2]).transpose(3, 0, 2, 1)

    def up_bias(name):
        b = _np.concatenate([a[ffn + "s" + name][None], a[ffn + name]])
        return b.reshape(b.shape[0], -1, 2).transpose(1, 0, 2)

    w_up = _np.stack([up("w3"), up("w1")], axis=3).reshape(128, 9, 4, 128)
    b_up = _np.stack([up_bias("b3"), up_bias("b1")], axis=3).reshape(128, 36)
    w_down = _np.concatenate([a[ffn + "sw2"][None], a[ffn + "w2"]]).transpose(2, 0, 1)
    attn_w = _np.stack([a[attn + "Wq"].T, a[attn + "Wk"].T, a[attn + "Wv"], a[attn + "Wo"].T], axis=1)
    cols = _np.concatenate([b_up] + [a[k][:, None] for k in (attn + "bq", attn + "bk", attn + "bv", ffn + "sb2")], axis=1)
    rows = _np.broadcast_to(_np.concatenate([a[attn + "bo"], a[ffn + "gate_b"]])[None], (128, 136))
    arrays = {
        "in_x": x.reshape(-1, x.shape[-1]), "in_w_up": w_up, "in_w_down": w_down, "in_attn_w": attn_w,
        "in_cols": cols, "in_rows": rows, "in_gate_w": a[ffn + "gate_w"].T,
        "in_b2rows": a[ffn + "b2"],
    }
    arrays = {k: _np.ascontiguousarray(v) for k, v in arrays.items()}
    nc = _bacc.Bacc("TRN2", target_bir_lowering=False, num_devices=1)
    args = [nc.dram_tensor(k, v.shape, _mybir.dt.from_np(v.dtype), kind="ExternalInput").ap()
            for k, v in arrays.items()]
    args.append(nc.dram_tensor("out", arrays["in_x"].shape, _mybir.dt.float32, kind="ExternalOutput").ap())
    block_kernel(nc, *args)
    r = _run(nc, [arrays], core_ids=[0])
    return r.results[0]["out"].reshape(x.shape)
```

```python
from contextlib import ExitStack

import concourse.bass as bass
from concourse import mybir

F32 = mybir.dt.float32
F32R = mybir.dt.float32r
ACT = mybir.ActivationFunctionType
ALU = mybir.AluOpType
AX_X = mybir.AxisListType.X

P = 128
D = 128
TOK = 512
CH = TOK // P
NR = 8
NE = NR + 1
LIMIT = 7.0
LN_EPS = 1e-5
DEN_EPS = 1e-6
ROUTE_STEPS = 7
LN_STEPS = 4
DVE_HI = 3, 6

C_BUP, C_BQ, C_BK, C_BV, C_SB2, N_COL = 0, 4 * NE, 4 * NE + 1, 4 * NE + 2, 4 * NE + 3, 4 * NE + 4


def block_kernel(nc, x_in, w_up, w_down, attn_w, cols, rows, gate_w, b2rows, out):
    NB = x_in.shape[0] // TOK
    x_b = x_in.rearrange("(b c p) d -> b p c d", c=CH, p=P)
    out_b = out.rearrange("(b c p) d -> b p c d", c=CH, p=P)

    cw_dram = nc.dram_tensor("cw_dram", [2, NR, TOK], F32, kind="Internal").ap()

    with ExitStack() as ctx:
        def sb(name, shape, dt=F32):
            return ctx.enter_context(nc.sbuf_tensor(name, shape, dt))

        def bank(name):
            return ctx.enter_context(nc.psum_tensor(name, [P, TOK], F32))

        def sem(name):
            return ctx.enter_context(nc.semaphore(name))

        up_f32 = sb("up_f32", [P, NE, 4, P])
        down_f32 = sb("down_f32", [P, NE, D])
        up_hi, up_lo = sb("up_hi", [P, NE, 4, P], F32R), sb("up_lo", [P, NE, 4, P], F32R)
        down_hi, down_lo = sb("down_hi", [P, NE, D], F32R), sb("down_lo", [P, NE, D], F32R)
        attn_sb = sb("attn_sb", [P, 4, P])
        wov = sb("wov", [P, D])
        bvo = sb("bvo", [P, D])
        bv_wide = sb("bv_wide", [P, P])
        col = sb("col", [P, N_COL])
        row = sb("row", [P, D + NR])
        gate_f32 = sb("gate_f32", [P, NR])
        gate_split = sb("gate_split", [P, 2, NR], F32R)
        b2_sb = sb("b2_sb", [NR, D])
        ident = sb("ident", [P, P])
        causal = sb("causal", [P, P])
        earlier = sb("earlier", [P, NR, NR])
        minus_half = sb("minus_half", [P, CH])

        x_sb = [sb(f"x_sb{i}", [P, CH, D]) for i in range(2)]
        stats1, mv1 = sb("stats1", [P, CH, 6]), sb("mv1", [P, 6, CH])
        stats2, mv2 = sb("stats2", [P, CH, 6]), sb("mv2", [P, 6, CH])
        var1, rstd1, shift1 = sb("var1", [P, CH]), sb("rstd1", [P, CH]), sb("shift1", [P, CH])
        var2, rstd2, shift2 = sb("var2", [P, CH]), sb("rstd2", [P, CH]), sb("shift2", [P, CH])
        xn = sb("xn", [P, CH, D])
        xnT = sb("xnT", [P, TOK])
        q_exp, q_relu, qf = sb("q_exp", [P, TOK]), sb("q_relu", [P, TOK]), sb("qf", [P, TOK])
        k_exp, k_relu, kf = sb("k_exp", [P, TOK]), sb("k_relu", [P, TOK]), sb("kf", [P, TOK])
        v1 = sb("v1", [P, CH, D + 1])
        a_diag = sb("a_diag", [P, CH, P])
        a_off = sb("a_off", [P, 6, P])
        x_bo = sb("x_bo", [P, CH, D])
        den, rden = sb("den", [P, CH]), sb("rden", [P, CH])
        y_sb = [sb(f"y_sb{i}", [P, CH, D]) for i in range(4)]
        yn = sb("yn", [P, CH, D])
        ynT_hi = [sb(f"ynT_hi{i}", [P, TOK], F32R) for i in range(2)]
        ynT_lo = [sb(f"ynT_lo{i}", [P, TOK], F32R) for i in range(2)]

        r_log = sb("r_log", [P, CH, NR])
        r_max, r_lg, r_ex = sb("r_max", [P, CH]), sb("r_lg", [P, CH, NR]), sb("r_ex", [P, CH, NR])
        r_sum, r_inv, r_sc = sb("r_sum", [P, CH]), sb("r_inv", [P, CH]), sb("r_sc", [P, CH, NR])
        r_b = sb("r_b", [P, CH, NR])
        r_gt, r_eq = sb("r_gt", [P, CH, NR, NR]), sb("r_eq", [P, CH, NR, NR])
        r_tie, r_before = sb("r_tie", [P, CH, NR, NR]), sb("r_before", [P, CH, NR, NR])
        r_place = sb("r_place", [P, CH, NR])
        r_cw = sb("r_cw", [P, CH, NR])
        cwT = [sb(f"cwT{i}", [NR, TOK]) for i in range(2)]
        cw_wide = sb("cw_wide", [P, NR, TOK])

        h3_sb = [[sb(f"h3_sb{i}{h}", [P, TOK]) for h in "gl"] for i in range(2)]
        gate_act = [sb(f"gate_act{i}", [P, TOK]) for i in range(2)]
        lin = [sb(f"lin{i}", [P, TOK]) for i in range(2)]
        glu = [sb(f"glu{i}", [P, TOK]) for i in range(2)]
        glu_w = [sb(f"glu_w{i}", [P, TOK]) for i in range(2)]
        act = [sb(f"act{i}", [P, TOK]) for i in range(2)]
        act_hi = [sb(f"act_hi{i}", [P, TOK], F32R) for i in range(2)]
        act_lo = [sb(f"act_lo{i}", [P, TOK], F32R) for i in range(2)]
        ffT = sb("ffT", [P, TOK])
        o_sb = [sb(f"o_sb{i}", [P, CH, D]) for i in range(2)]

        h_bank = [bank(f"h_bank{k}") for k in range(4)]
        ff_bank = bank("ff_bank")
        misc_bank = bank("misc_bank")
        at_bank = [bank(f"at_bank{k}") for k in range(2)]

        w_loaded = [sem(f"w_loaded{e}") for e in range(NE)]
        c_loaded, aw_loaded = sem("c_loaded"), sem("aw_loaded")
        x_loaded = [sem("x_loaded0"), sem("x_loaded1")]
        o_stored = [sem("o_stored0"), sem("o_stored1")]
        pool_const, dve_const = sem("pool_const"), sem("dve_const")
        w_hi_done, w_lo_done = sem("w_hi_done"), sem("w_lo_done")
        wov_mm, wov_ready = sem("wov_mm"), sem("wov_ready")
        ln1_step, ln2_step, route_step, den_step = (sem("ln1_step"), sem("ln2_step"),
                                                    sem("route_step"), sem("den_step"))
        rstd1_done, rstd2_done = sem("rstd1_done"), sem("rstd2_done")
        xn_ready, t1_done, xnT_ready = sem("xn_ready"), sem("t1_done"), sem("xnT_ready")
        q_mm, k_mm, v_mm = sem("q_mm"), sem("k_mm"), sem("v_mm")
        q_read, k_read = sem("q_read"), sem("k_read")
        qk_ready, v_ready = sem("qk_ready"), sem("v_ready")
        diag_mm, off_mm, off2_mm = sem("diag_mm"), sem("off_mm"), sem("off2_mm")
        diag_ready, off_ready, off2_ready = sem("diag_ready"), sem("off_ready"), sem("off2_ready")
        xbo_ready, num_mm, y_ready = sem("xbo_ready"), sem("num_mm"), sem("y_ready")
        yn_ready, t2_done = sem("yn_ready"), sem("t2_done")
        ynT_hi_ready, ynT_lo_ready = sem("ynT_hi_ready"), sem("ynT_lo_ready")
        gate_mm, lg_ready, ex_ready = sem("gate_mm"), sem("lg_ready"), sem("ex_ready")
        biased_ready, compared = sem("biased_ready"), sem("compared")
        order_step, before_ready = sem("order_step"), sem("before_ready")
        cw_ready, cwT_mm, cwT_ready = sem("cw_ready"), sem("cwT_mm"), sem("cwT_ready")
        h_ready, h3_copied, h_used = sem("h_ready"), sem("h3_copied"), sem("h_used")
        ga_ready, lin_ready, glu_ready = sem("ga_ready"), sem("lin_ready"), sem("glu_ready")
        cw_written, gluw_ready = sem("cw_written"), sem("gluw_ready")
        cw_loaded = [sem(f"cw_loaded{e}") for e in range(NR)]
        act_ready, act_hi_ready, act_lo_ready = sem("act_ready"), sem("act_hi_ready"), sem("act_lo_ready")
        down_done, ff_copied = sem("down_done"), sem("ff_copied")
        ffo_mm, o_ready = sem("ffo_mm"), sem("o_ready")

        OFF = [(0, 1), (0, 2), (0, 3), (2, 3), (1, 2), (1, 3)]

        def walk(eng, body):
            body(-2, 2, -1, False, False, False, True)
            body(-1, 3, -1, False, False, True, True)
            body(0, 0, 0, True, False, True, True)
            with eng.Fori(0, (NB - 4) // 4) as i:
                for j in range(1, 5):
                    body(4 * i + j, j % 4, 2 * i + j // 2, True, True, True, True)
            body(NB - 3, 1, (NB - 3) // 2, True, True, True, True)
            body(NB - 2, 2, (NB - 2) // 2, True, True, True, False)
            body(NB - 1, 3, (NB - 1) // 2, True, True, False, False)
            body(NB, 0, NB // 2, False, True, False, False)

        ROUTE_AT = {(6, 2): 0, (6, 3): 1, (6, 4): 2, (7, 4): 3, (8, 1): 4}

        block = ctx.enter_context(nc.Block())

        @block.sync
        def _(sp):
            sp.dma_start(x_sb[0][:], x_b[0]).then_inc(x_loaded[0], 16)
            sp.dma_start(col[:], cols).then_inc(c_loaded, 16)
            sp.dma_start(attn_sb[:], attn_w).then_inc(aw_loaded, 16)
            sp.dma_start(row[:], rows).then_inc(c_loaded, 16)
            sp.dma_start(gate_f32[:], gate_w).then_inc(c_loaded, 16)
            sp.dma_start(b2_sb[:], b2rows).then_inc(c_loaded, 16)
            sp.dma_start(x_sb[1][:], x_b[1]).then_inc(x_loaded[1], 16)
            for e in range(NE):
                sp.dma_start(up_f32[:, e], w_up[:, e]).then_inc(w_loaded[e], 16)
                sp.dma_start(down_f32[:, e], w_down[:, e]).then_inc(w_loaded[e], 16)

            def body(n, q, h, ff, old, late, early):
                par = q % 2
                if ff:
                    sp.wait_ge(cwT_ready, n + 1)
                    sp.dma_start(cw_dram[par], cwT[par][:]).then_inc(cw_written, 16)
                    sp.wait_ge(cw_written, 16 * n + 16)
                    for e in range(NR):
                        if not (isinstance(n, int) and n == 0):
                            sp.wait_ge(gluw_ready, NR * n - NR + e + 1)
                        sp.dma_start(cw_wide[:, e], cw_dram[par, e:e + 1].broadcast_to([P, TOK])).then_inc(cw_loaded[e], 16)
                if early and not (isinstance(n, int) and (n < -1 or n + 3 >= NB)):
                    sp.wait_ge(xbo_ready, n + 2)
                    sp.wait_ge(xn_ready, n + 2)
                    sp.dma_start(x_sb[1 - par][:], x_b[n + 3]).then_inc(x_loaded[1 - par], 16)
                if old:
                    sp.wait_ge(o_ready, n)
                    sp.dma_start(out_b[n - 1], o_sb[1 - par][:]).then_inc(o_stored[1 - par], 16)

            walk(sp, body)
            for i in range(2):
                sp.wait_ge(o_stored[i], 16 * (NB // 2))

        @block.scalar
        def _(act_e):
            def split_hi(e):
                act_e.wait_ge(w_loaded[e], 32)
                act_e.activation(up_hi[:, e], up_f32[:, e], ACT.Copy).then_inc(w_hi_done, 1)
                act_e.activation(down_hi[:, e], down_f32[:, e], ACT.Copy).then_inc(w_hi_done, 1)

            def normalize(dst, src, rstd, shift, ready):
                for c in range(CH):
                    i = act_e.activation(dst[:, c], src[:, c], ACT.Identity, bias=shift[:, c:c + 1],
                                         scale=rstd[:, c:c + 1])
                i.then_inc(ready, 1)

            act_e.wait_ge(wov_mm, 1)
            act_e.activation(wov[:], at_bank[1][:, 0:D], ACT.Copy).then_inc(wov_ready, 1)
            act_e.activation(bvo[:], at_bank[1][:, D:2 * D], ACT.Copy).then_inc(wov_ready, 1)

            def body(n, q, h, ff, old, late, early):
                par = q % 2
                m = n + 1
                for e in range(NE):
                    u, r = 9 * n + e, (par + e) % 2
                    if ff:
                        act_e.wait_ge(h_ready, 4 * u + 1)
                        act_e.activation(h3_sb[r][0][:], h_bank[0][:], ACT.Identity,
                                         bias=col[:, 4 * e:4 * e + 1]).then_inc(h3_copied, 1)
                    if early and e == 8:
                        act_e.wait_ge(off_mm, m + 2)
                        if late:
                            act_e.wait_ge(num_mm, 2 * m + 2)
                        act_e.activation(a_off[:, 0:4], at_bank[1][:].rearrange("p (k t) -> p k t", t=P),
                                         ACT.Copy).then_inc(off_ready, 1)
                    if late and e == 0:
                        act_e.wait_ge(off2_mm, m + 1)
                        act_e.activation(a_off[:, 4:6], at_bank[0][:, 0:2 * P].rearrange("p (k t) -> p k t", t=P),
                                         ACT.Copy).then_inc(off2_ready, 1)
                    if late and e == 4:
                        act_e.wait_ge(t2_done, m + 1)
                        act_e.activation(ynT_hi[1 - par][:], at_bank[1][:], ACT.Copy).then_inc(ynT_hi_ready, 1)
                    if late and e == 3:
                        act_e.wait_ge(rstd2_done, 2 * m + 2)
                        if not (isinstance(m, int) and m < 1):
                            act_e.wait_ge(t2_done, m)
                        normalize(yn, y_sb[(q + 1) % 4], rstd2, shift2, yn_ready)
                    if early and e == 3:
                        act_e.wait_ge(t1_done, m + 2)
                        if late:
                            act_e.wait_ge(v_mm, m + 1)
                        act_e.activation(xnT[:], at_bank[0][:], ACT.Copy).then_inc(xnT_ready, 1)
                    if ff:
                        act_e.wait_ge(h_ready, 4 * u + 3)
                        act_e.activation(h3_sb[r][1][:], h_bank[2][:], ACT.Identity,
                                         bias=col[:, 4 * e + 2:4 * e + 3]).then_inc(h3_copied, 1)
                    if late and e == 6:
                        act_e.wait_ge(lg_ready, m + 1)
                        act_e.activation(r_ex[:], r_lg[:], ACT.Exp).then_inc(ex_ready, 1)
                    if early and e == 6:
                        act_e.activation(q_exp[:], at_bank[1][:], ACT.Exp,
                                         bias=col[:, C_BQ:C_BQ + 1]).then_inc(q_read, 1)
                        act_e.activation(k_exp[:], at_bank[0][:], ACT.Exp,
                                         bias=col[:, C_BK:C_BK + 1]).then_inc(k_read, 1)
                    if ff and e == 0:
                        act_e.wait_ge(cwT_mm, n + 1)
                        act_e.activation(cwT[par][:], misc_bank[0:NR, :], ACT.Copy).then_inc(cwT_ready, 1)
                    if ff and e > 0 and e not in DVE_HI or old and e == 0:
                        act_e.wait_ge(act_ready, u)
                        if not (isinstance(u, int) and u < 3):
                            act_e.wait_ge(down_done, u - 2)
                        act_e.activation(act_hi[1 - r][:], act[1 - r][:], ACT.Copy).then_inc(act_hi_ready, 1)
                    if ff:
                        act_e.wait_ge(ga_ready, u + 1)
                        act_e.activation(glu[r][:], gate_act[r][:],
                                         ACT.Gelu_apprx_sigmoid).then_inc(glu_ready, 1)
                    if old and e == 1:
                        act_e.wait_ge(down_done, NE * n)
                        act_e.activation(ffT[:], ff_bank[:], ACT.Identity,
                                         bias=col[:, C_SB2:C_SB2 + 1]).then_inc(ff_copied, 1)
                    if early and e == 0:
                        act_e.wait_ge(rstd1_done, 2 * m + 4)
                        if late:
                            act_e.wait_ge(t1_done, m + 1)
                        normalize(xn, x_sb[par], rstd1, shift1, xn_ready)
                    if early and e == 5:
                        act_e.wait_ge(k_mm, m + 2)
                        act_e.wait_ge(q_mm, m + 2)
                        if late:
                            act_e.wait_ge(qk_ready, 2 * m + 2)
                        act_e.activation(q_relu[:], at_bank[1][:], ACT.Relu,
                                         bias=col[:, C_BQ:C_BQ + 1]).then_inc(q_read, 1)
                        act_e.activation(k_relu[:], at_bank[0][:], ACT.Relu,
                                         bias=col[:, C_BK:C_BK + 1]).then_inc(k_read, 1)
                    if isinstance(n, int) and n == -1:
                        split_hi(e)

            walk(act_e, body)

        @block.vector
        def _(dve):
            def chunk_bc(small):
                return small.unsqueeze(2).to_broadcast([P, CH, NR])

            def norm_stats(src, stats, mv, var, step, m, used):
                for c in range(CH):
                    i = dve.bn_stats(stats[:, c], src[:, c])
                i.then_inc(step, 1)
                if not (isinstance(m, int) and m < 1):
                    dve.wait_ge(used, 2 * m)
                dve.wait_ge(step, LN_STEPS * m + 1)
                dve.tensor_tensor(mv[:, 0], stats[:, :, 1], stats[:, :, 4], ALU.add)
                dve.tensor_tensor(mv[:, 1], stats[:, :, 1], stats[:, :, 4], ALU.subtract)
                dve.tensor_tensor(mv[:, 2], stats[:, :, 2], stats[:, :, 5], ALU.add).then_inc(step, 1)
                dve.wait_ge(step, LN_STEPS * m + 2)
                dve.tensor_scalar(mv[:, 3], mv[:, 0], -0.5, None, ALU.mult)
                dve.tensor_scalar(mv[:, 5], mv[:, 2], 1.0 / D, LN_EPS, ALU.mult, ALU.add)
                dve.scalar_tensor_tensor(mv[:, 4], mv[:, 1], 0.25, mv[:, 1], ALU.mult, ALU.mult).then_inc(step, 1)
                dve.wait_ge(step, LN_STEPS * m + 3)
                dve.tensor_tensor(var[:], mv[:, 4], mv[:, 5], ALU.add).then_inc(step, 1)

            def routing_scores(m):
                dve.wait_ge(gate_mm, m + 1)
                lg = misc_bank[:, 0:2 * CH * NR].rearrange("p (c k r) -> p c k r", k=2, r=NR)
                dve.tensor_copy(r_lg[:], lg[:, :, 1]).then_inc(route_step, 1)
                dve.wait_ge(route_step, ROUTE_STEPS * m + 1)
                dve.tensor_tensor(r_log[:], lg[:, :, 0], r_lg[:], ALU.add).then_inc(route_step, 1)
                dve.wait_ge(route_step, ROUTE_STEPS * m + 2)
                dve.reduce_max(r_max[:], r_log[:], AX_X).then_inc(route_step, 1)
                dve.wait_ge(route_step, ROUTE_STEPS * m + 3)
                dve.tensor_tensor(r_lg[:], r_log[:], chunk_bc(r_max[:]), ALU.subtract).then_inc(lg_ready, 1)

            def routing_choice(m, piece):
                def after(i):
                    dve.wait_ge(route_step, ROUTE_STEPS * m + i)

                if piece == 0:
                    dve.wait_ge(ex_ready, m + 1)
                    dve.reduce_sum(r_sum[:], r_ex[:], AX_X).then_inc(route_step, 1)
                    after(4)
                    dve.reciprocal(r_inv[:], r_sum[:]).then_inc(route_step, 1)
                if piece == 1:
                    after(5)
                    dve.tensor_tensor(r_sc[:], r_ex[:], chunk_bc(r_inv[:]), ALU.mult).then_inc(route_step, 1)
                    after(6)
                    dve.tensor_tensor(r_b[:], r_sc[:], row[:, D:D + NR].unsqueeze(1).to_broadcast([P, CH, NR]),
                                      ALU.add).then_inc(biased_ready, 1)
                if piece == 2:
                    mine = r_b[:].unsqueeze(3).to_broadcast([P, CH, NR, NR])
                    other = r_b[:].unsqueeze(2).to_broadcast([P, CH, NR, NR])
                    dve.wait_ge(biased_ready, m + 1)
                    dve.tensor_tensor(r_gt[:], other, mine, ALU.is_gt)
                    dve.tensor_tensor(r_eq[:], other, mine, ALU.is_equal).then_inc(compared, 1)
                if piece == 3:
                    dve.wait_ge(before_ready, m + 1)
                    dve.reduce_sum(r_place[:], r_before[:], AX_X).then_inc(route_step, 1)
                if piece == 4:
                    after(7)
                    dve.scalar_tensor_tensor(r_cw[:], r_place[:], 2.0, r_sc[:], ALU.is_lt, ALU.mult).then_inc(cw_ready, 1)
            def body(n, q, h, ff, old, late, early):
                par = q % 2
                m = n + 1
                ahead = not (isinstance(n, int) and n + 3 >= NB)
                y = y_sb[(q + 1) % 4]
                for e in range(NE):
                    u, r = 9 * n + e, (par + e) % 2

                    def routing(place):
                        if late and (e, place) in ROUTE_AT:
                            routing_choice(m, ROUTE_AT[e, place])

                    if early and e == 8:
                        dve.wait_ge(diag_mm, m + 2)
                        if late:
                            dve.wait_ge(num_mm, 2 * m + 2)
                        dve.tensor_tensor(a_diag[:], at_bank[0][:].rearrange("p (c t) -> p c t", t=P),
                                          causal[:].unsqueeze(1).to_broadcast([P, CH, P]), ALU.mult).then_inc(diag_ready, 1)
                    if old and e == 3:
                        dve.wait_ge(ffo_mm, n)
                        if not (isinstance(n, int) and n < 3):
                            dve.wait_ge(o_stored[1 - par], 16 * (h - (1 if par == 0 else 0)))
                        dve.tensor_tensor(o_sb[1 - par][:], misc_bank[:].rearrange("p (c d) -> p c d", d=D),
                                          y_sb[(q + 3) % 4][:], ALU.add).then_inc(o_ready, 1)
                    if late and e == 1:
                        o = [at_bank[1 - g][:, 0:2 * (D + 1)].rearrange("p (c d) -> p c d", d=D + 1) for g in range(2)]
                        for g in range(2):
                            dve.wait_ge(num_mm, 2 * m + g + 1)
                            i = dve.tensor_scalar(den[:, 2 * g:2 * g + 2], o[g][:, :, D], DEN_EPS, None, ALU.add)
                        i.then_inc(den_step, 1)
                        dve.wait_ge(den_step, 2 * m + 1)
                        dve.reciprocal(rden[:], den[:]).then_inc(den_step, 1)
                        dve.wait_ge(den_step, 2 * m + 2)
                        dve.wait_ge(xbo_ready, m + 1)
                        for c in range(CH):
                            i = dve.scalar_tensor_tensor(y[:, c], o[c // 2][:, c % 2, 0:D], rden[:, c:c + 1], x_bo[:, c],
                                                         ALU.mult, ALU.add)
                        i.then_inc(y_ready, 1)
                    if late and e == 5:
                        routing_scores(m)
                    if ahead and e == 5:
                        dve.wait_ge(x_loaded[1 - par], 16 * (h + 2 + par))
                        norm_stats(x_sb[1 - par], stats1, mv1, var1, ln1_step, m + 2, rstd1_done)
                    if early and e == 6:
                        dve.wait_ge(v_mm, m + 2)
                        if late:
                            dve.wait_ge(num_mm, 2 * m + 2)
                        dve.tensor_tensor(v1[:, :, 0:D], misc_bank[:].rearrange("p (c d) -> p c d", d=D),
                                          bvo[:].unsqueeze(1).to_broadcast([P, CH, D]), ALU.add).then_inc(v_ready, 1)
                    if ff:
                        dve.wait_ge(h3_copied, 2 * u + 1)
                        dve.wait_ge(h_ready, 4 * u + 2)
                        dve.scalar_tensor_tensor(gate_act[r][:], h_bank[1][:], col[:, 4 * e + 1:4 * e + 2],
                                                 h3_sb[r][0][:], ALU.add, ALU.mult).then_inc(h_used, 1)
                    routing(0)
                    if late and e == 4:
                        dve.wait_ge(t2_done, m + 1)
                        dve.wait_ge(ynT_hi_ready, m + 1)
                        dve.tensor_tensor(ynT_lo[1 - par][:], at_bank[1][:], ynT_hi[1 - par][:].bitcast(F32),
                                          ALU.subtract).then_inc(ynT_lo_ready, 1)
                    if ff and e > 0 or old and e == 0:
                        dve.wait_ge(lin_ready, u)
                        if e == 1:
                            dve.wait_ge(glu_ready, u)
                            if not (isinstance(u, int) and u < 3):
                                dve.wait_ge(act_lo_ready, u - 2)
                            src = glu
                        else:
                            dve.wait_ge(gluw_ready, NR * n + (e - 1 if e else 0))
                            src = glu_w
                        dve.scalar_tensor_tensor(act[1 - r][:], lin[1 - r][:], 1.0, src[1 - r][:],
                                                 ALU.add, ALU.mult).then_inc(act_ready, 1)
                    if ff and e in DVE_HI:
                        dve.wait_ge(act_ready, u)
                        dve.wait_ge(act_hi_ready, u - 1)
                        if not (isinstance(u, int) and u < 3):
                            dve.wait_ge(down_done, u - 2)
                        dve.tensor_copy(act_hi[1 - r][:], act[1 - r][:]).then_inc(act_hi_ready, 1)
                    routing(1)
                    if ff:
                        dve.wait_ge(h_used, 2 * u + 1)
                        dve.tensor_scalar(gate_act[r][:], gate_act[r][:], LIMIT, None, ALU.min).then_inc(ga_ready, 1)
                    routing(2)
                    if ff:
                        dve.wait_ge(h3_copied, 2 * u + 2)
                        dve.wait_ge(h_ready, 4 * u + 4)
                        dve.scalar_tensor_tensor(lin[r][:], h_bank[3][:], col[:, 4 * e + 3:4 * e + 4],
                                                 h3_sb[r][1][:], ALU.add, ALU.mult).then_inc(h_used, 1)
                    if early and e == 6:
                        dve.wait_ge(q_read, 2 * m + 4)
                        if late:
                            dve.wait_ge(off2_mm, m + 1)
                        dve.scalar_tensor_tensor(qf[:], q_exp[:], 1.0, q_relu[:], ALU.min, ALU.add).then_inc(qk_ready, 1)
                        dve.wait_ge(k_read, 2 * m + 4)
                        dve.scalar_tensor_tensor(kf[:], k_exp[:], 1.0, k_relu[:], ALU.min, ALU.add).then_inc(qk_ready, 1)
                    routing(3)
                    if late and e == 1:
                        dve.wait_ge(y_ready, m + 1)
                        norm_stats(y, stats2, mv2, var2, ln2_step, m, rstd2_done)
                    if ff:
                        dve.wait_ge(h_used, 2 * u + 2)
                        dve.tensor_scalar(lin[r][:], lin[r][:], LIMIT, -LIMIT, ALU.min, ALU.max).then_inc(lin_ready, 1)
                    routing(4)

            dve.wait_ge(x_loaded[0], 16)
            norm_stats(x_sb[0], stats1, mv1, var1, ln1_step, 0, rstd1_done)
            dve.wait_ge(c_loaded, 64)
            dve.tensor_copy(bv_wide[:], col[:, C_BV:C_BV + 1].to_broadcast([P, P])).then_inc(dve_const, 1)
            dve.tensor_copy(gate_split[:, 0], gate_f32[:]).then_inc(dve_const, 1)
            dve.wait_ge(dve_const, 2)
            dve.tensor_tensor(gate_split[:, 1], gate_f32[:], gate_split[:, 0].bitcast(F32), ALU.subtract).then_inc(dve_const, 1)
            dve.wait_ge(pool_const, 8)
            walk(dve, body)

        @block.gpsimd
        def _(pool):
            def ones_where_zero(t, base, pattern, chan, count):
                pool.wait_ge(pool_const, count)
                pool.affine_select(out=t, in_=t, compare_op=ALU.not_equal, fill=1.0, base=base,
                                   pattern=pattern, channel_multiplier=chan).then_inc(pool_const, 1)

            pool.memset(minus_half[:], -0.5).then_inc(pool_const, 1)
            pool.memset(ident[:], 0.0).then_inc(pool_const, 1)
            pool.memset(causal[:], 1.0).then_inc(pool_const, 1)
            pool.memset(v1[:], 1.0).then_inc(pool_const, 1)
            ones_where_zero(ident[:], 0, [[-1, P]], 1, 2)
            pool.memset(earlier[:], 1.0).then_inc(pool_const, 1)
            pool.wait_ge(pool_const, 3)
            pool.affine_select(out=causal[:], in_=causal[:], compare_op=ALU.is_ge, fill=0.0, base=0,
                               pattern=[[1, P]], channel_multiplier=-1).then_inc(pool_const, 1)
            pool.wait_ge(pool_const, 6)
            pool.affine_select(out=earlier[:], in_=earlier[:], compare_op=ALU.is_ge, fill=0.0, base=-1,
                               pattern=[[1, NR], [-1, NR]], channel_multiplier=0).then_inc(pool_const, 1)

            def rsqrt(var, mv, rstd, shift, step, m, done, used):
                pool.wait_ge(step, LN_STEPS * (m + 1))
                if not (isinstance(m, int) and m < 1):
                    pool.wait_ge(used, m)
                pool.tensor_tensor(rstd[:], var[:], minus_half[:], ALU.pow).then_inc(done, 1)
                pool.wait_ge(done, 2 * m + 1)
                pool.tensor_tensor(shift[:], mv[:, 3], rstd[:], ALU.mult).then_inc(done, 1)

            def weigh(n, e, u, r):
                pool.wait_ge(glu_ready, u + 1)
                pool.wait_ge(cw_loaded[e - 1], 16 * n + 16)
                pool.tensor_tensor(glu_w[r][:], glu[r][:], cw_wide[:, e - 1], ALU.mult).then_inc(gluw_ready, 1)

            def body(n, q, h, ff, old, late, early):
                par = q % 2
                ahead = not (isinstance(n, int) and n + 3 >= NB)
                m = n + 1
                for e in range(NE):
                    u, r = 9 * n + e, (par + e) % 2
                    if late and e == 2:
                        rsqrt(var2, mv2, rstd2, shift2, ln2_step, m, rstd2_done, yn_ready)
                    if isinstance(n, int) and n == -2 and e == 0:
                        rsqrt(var1, mv1, rstd1, shift1, ln1_step, 0, rstd1_done, xn_ready)
                    if ahead and e == 6:
                        rsqrt(var1, mv1, rstd1, shift1, ln1_step, m + 2, rstd1_done, xn_ready)
                    weigh_first = isinstance(n, int) and n == NB - 1 and e >= 2
                    if weigh_first:
                        weigh(n, e, u, r)
                    if ff and e > 0 or old and e == 0:
                        pool.wait_ge(act_hi_ready, u)
                        pool.tensor_tensor(act_lo[1 - r][:], act[1 - r][:], act_hi[1 - r][:].bitcast(F32),
                                           ALU.subtract).then_inc(act_lo_ready, 1)
                    if ff and e >= 1 and not weigh_first:
                        weigh(n, e, u, r)
                    if early and e == 8:
                        if isinstance(n, int) and n == -2:
                            pool.wait_ge(c_loaded, 64)
                        if late:
                            pool.wait_ge(y_ready, m + 1)
                        pool.tensor_tensor(x_bo[:], x_sb[par][:], row[:, 0:D].unsqueeze(1).to_broadcast([P, CH, D]),
                                           ALU.add).then_inc(xbo_ready, 1)
                    if late and e == 6:
                        pool.wait_ge(compared, m + 1)
                        for c in range(CH):
                            i = pool.tensor_tensor(r_tie[:, c], r_eq[:, c], earlier[:], ALU.mult)
                        i.then_inc(order_step, 1)
                        pool.wait_ge(order_step, m + 1)
                        pool.tensor_tensor(r_before[:], r_gt[:], r_tie[:], ALU.add).then_inc(before_ready, 1)
                    if isinstance(n, int) and n == -1:
                        pool.wait_ge(w_hi_done, 2 * e + 2)
                        pool.tensor_tensor(up_lo[:, e], up_f32[:, e], up_hi[:, e].bitcast(F32), ALU.subtract).then_inc(w_lo_done, 1)
                        pool.tensor_tensor(down_lo[:, e], down_f32[:, e], down_hi[:, e].bitcast(F32), ALU.subtract).then_inc(w_lo_done, 1)

            walk(pool, body)

        @block.tensor
        def _(pe):
            def three(out_ap, w_hi, w_lo, x_hi, x_lo, start=True, stop=True):
                pe.matmul(out_ap, w_hi, x_hi, start=start, stop=False)
                pe.matmul(out_ap, w_hi, x_lo, start=False, stop=False)
                return pe.matmul(out_ap, w_lo, x_hi, start=False, stop=stop)

            def transposes(dst, src):
                for c in range(CH):
                    i = pe.transpose(dst[:, c * P:(c + 1) * P], src(c), ident[:])
                return i

            pe.wait_ge(aw_loaded, 16)
            pe.wait_ge(dve_const, 1)
            pe.matmul(at_bank[1][:, 0:D], attn_sb[:, 2], attn_sb[:, 3], start=True, stop=True)
            pe.matmul(at_bank[1][:, D:2 * D], bv_wide[:], attn_sb[:, 3], start=True, stop=True).then_inc(wov_mm, 1)

            def scores(dst, s, t):
                return pe.matmul(dst, kf[:, s * P:(s + 1) * P], qf[:, t * P:(t + 1) * P], start=True, stop=True)

            pe.wait_ge(pool_const, 5)

            def up(n, par, e):
                u = 9 * n + e
                if e == 0:
                    pe.wait_ge(ynT_hi_ready, n + 1)
                    pe.wait_ge(ynT_lo_ready, n + 1)
                if isinstance(n, int) and n == 0:
                    pe.wait_ge(w_lo_done, 2 * e + 2)
                for k in range(4):
                    if not (isinstance(u, int) and u == 0):
                        pe.wait_ge(h_used if k % 2 else h3_copied, 2 * u - 1 + k // 2)
                    three(h_bank[k][:], up_hi[:, e, k], up_lo[:, e, k], ynT_hi[par][:],
                          ynT_lo[par][:]).then_inc(h_ready, 1)

            def down(n, par, e):
                pe.wait_ge(act_lo_ready, 9 * n + e + 1)
                if e == 0:
                    if not (isinstance(n, int) and n == 0):
                        pe.wait_ge(ff_copied, n)
                    pe.wait_ge(cwT_ready, n + 1)
                    pe.matmul(ff_bank[:], b2_sb[:], cwT[par][:], start=True, stop=False)
                r = (par + e) % 2
                three(ff_bank[:], down_hi[:, e], down_lo[:, e], act_hi[r][:], act_lo[r][:],
                      start=False, stop=(e == NE - 1)).then_inc(down_done, 1)

            def batch_rows(n):
                pe.wait_ge(ff_copied, n)
                transposes(misc_bank, lambda c: ffT[:, c * P:(c + 1) * P]).then_inc(ffo_mm, 1)

            def logits(n, par):
                pe.wait_ge(ynT_lo_ready, n + 2)
                if isinstance(n, int) and n == -1:
                    pe.wait_ge(dve_const, 3)
                elif not (isinstance(n, int) and n == 0):
                    pe.wait_ge(o_ready, n)
                for c in range(CH):
                    t = slice(c * P, (c + 1) * P)
                    dst = misc_bank[:, 2 * NR * c:2 * NR * (c + 1)]
                    pe.matmul(dst, ynT_hi[1 - par][:, t], gate_split[:].rearrange("p k r -> p (k r)"), start=True, stop=False)
                    i = pe.matmul(dst[:, 0:NR], ynT_lo[1 - par][:, t], gate_split[:, 0], start=False, stop=True)
                i.then_inc(gate_mm, 1)

            def body(n, q, h, ff, old, late, early):
                par = q % 2
                m = n + 1
                for e in range(NE):
                    if ff and not (isinstance(n, int) and n == 0 and e == 0):
                        up(n, par, e)
                    if ff and e == 0:
                        pe.wait_ge(cw_ready, n + 1)
                        if not (isinstance(n, int) and n + 1 >= NB):
                            pe.wait_ge(v_ready, n + 2)
                        for c in range(CH):
                            i = pe.transpose(misc_bank[0:NR, c * P:(c + 1) * P], r_cw[:, c], ident[:])
                        i.then_inc(cwT_mm, 1)
                    if ff and e >= 2:
                        down(n, par, e - 2)
                    if old and e < 2:
                        down(n - 1, 1 - par, NE - 2 + e)
                    if late and e == 0:
                        pe.wait_ge(v_ready, m + 1)
                        pe.wait_ge(off_ready, m + 1)
                        pe.wait_ge(off2_ready, m + 1)
                        for c in range(CH):
                            dst = at_bank[1 - c // 2][:, (c % 2) * (D + 1):(c % 2 + 1) * (D + 1)]
                            for s in range(c + 1):
                                w = a_diag[:, c] if s == c else a_off[:, OFF.index((s, c))]
                                i = pe.matmul(dst, w, v1[:, s], start=(s == 0), stop=(s == c))
                            if c % 2:
                                i.then_inc(num_mm, 1)
                    if old and e == 2:
                        batch_rows(n)
                    if early and e == 2:
                        if late:
                            pe.wait_ge(y_ready, m + 1)
                        pe.wait_ge(xn_ready, m + 2)
                        transposes(at_bank[0], lambda c: xn[:, c]).then_inc(t1_done, 1)
                    if late and e == 3:
                        pe.wait_ge(yn_ready, m + 1)
                        transposes(at_bank[1], lambda c: yn[:, c]).then_inc(t2_done, 1)
                    if early and e == 4:
                        pe.wait_ge(xnT_ready, m + 2)
                        if isinstance(n, int) and n == -2:
                            pe.wait_ge(wov_ready, 2)
                        pe.matmul(at_bank[0][:], attn_sb[:, 1], xnT[:], start=True, stop=True).then_inc(k_mm, 1)
                    if late and e == 4:
                        logits(n, par)
                    if early and e == 4:
                        if late:
                            pe.wait_ge(ynT_lo_ready, m + 1)
                        pe.matmul(at_bank[1][:], attn_sb[:, 0], xnT[:], start=True, stop=True).then_inc(q_mm, 1)
                    if early and e == 5:
                        if late:
                            pe.wait_ge(lg_ready, m + 1)
                        for c in range(CH):
                            i = pe.matmul(misc_bank[:, c * D:(c + 1) * D], xnT[:, c * P:(c + 1) * P], wov[:],
                                          start=True, stop=True)
                        i.then_inc(v_mm, 1)
                    if isinstance(n, int) and n == -1 and e == 5:
                        up(0, 0, 0)
                    if early and e == 7:
                        pe.wait_ge(qk_ready, 2 * m + 4)
                        for c in range(CH):
                            i = scores(at_bank[0][:, c * P:(c + 1) * P], c, c)
                        i.then_inc(diag_mm, 1)
                        pe.wait_ge(k_read, 2 * m + 4)
                        for k in range(4):
                            i = scores(at_bank[1][:, k * P:(k + 1) * P], *OFF[k])
                        i.then_inc(off_mm, 1)
                    if early and e == 8:
                        pe.wait_ge(diag_ready, m + 2)
                        for k in range(2):
                            i = scores(at_bank[0][:, k * P:(k + 1) * P], *OFF[4 + k])
                        i.then_inc(off2_mm, 1)
            walk(pe, body)


def kernel(**inputs):
    import numpy as _np
    import concourse.bacc as _bacc
    from concourse import mybir as _mybir
    from concourse.bass_utils import run_bass_kernel_spmd as _run

    a = {k: _np.asarray(v) for k, v in inputs.items()}
    ffn, attn = "L0_ffn_", "L0_attn_"
    x = a[attn + "chunk"]

    def up(name):
        w = _np.concatenate([a[ffn + "s" + name][None], a[ffn + name]])
        return w.reshape(w.shape[0], -1, 2, w.shape[2]).transpose(3, 0, 2, 1)

    def up_bias(name):
        b = _np.concatenate([a[ffn + "s" + name][None], a[ffn + name]])
        return b.reshape(b.shape[0], -1, 2).transpose(1, 0, 2)

    w_up = _np.stack([up("w3"), up("w1")], axis=3).reshape(128, 9, 4, 128)
    b_up = _np.stack([up_bias("b3"), up_bias("b1")], axis=3).reshape(128, 36)
    w_down = _np.concatenate([a[ffn + "sw2"][None], a[ffn + "w2"]]).transpose(2, 0, 1)
    attn_w = _np.stack([a[attn + "Wq"].T, a[attn + "Wk"].T, a[attn + "Wv"], a[attn + "Wo"].T], axis=1)
    cols = _np.concatenate([b_up] + [a[k][:, None] for k in (attn + "bq", attn + "bk", attn + "bv", ffn + "sb2")], axis=1)
    rows = _np.broadcast_to(_np.concatenate([a[attn + "bo"], a[ffn + "gate_b"]])[None], (128, 136))
    arrays = {
        "in_x": x.reshape(-1, x.shape[-1]), "in_w_up": w_up, "in_w_down": w_down, "in_attn_w": attn_w,
        "in_cols": cols, "in_rows": rows, "in_gate_w": a[ffn + "gate_w"].T,
        "in_b2rows": a[ffn + "b2"],
    }
    arrays = {k: _np.ascontiguousarray(v) for k, v in arrays.items()}
    nc = _bacc.Bacc("TRN2", target_bir_lowering=False, num_devices=1)
    args = [nc.dram_tensor(k, v.shape, _mybir.dt.from_np(v.dtype), kind="ExternalInput").ap()
            for k, v in arrays.items()]
    args.append(nc.dram_tensor("out", arrays["in_x"].shape, _mybir.dt.float32, kind="ExternalOutput").ap())
    block_kernel(nc, *args)
    r = _run(nc, [arrays], core_ids=[0])
    return r.results[0]["out"].reshape(x.shape)
```
